# Optimizing a Trainium2 kernel written in Bass

```python
import numpy as np
import jax
import jax.numpy as jnp

def _softmax(x, axis=-1):
    return jax.nn.softmax(x, axis=axis)

def _gelu(x):
    return jax.nn.gelu(x, approximate=True)

def _silu(x):
    return jax.nn.silu(x)

def _sigmoid(x):
    return jax.nn.sigmoid(x)

def _layernorm(x, axis=-1, eps=1e-05):
    m = jnp.mean(x, axis=axis, keepdims=True)
    v = jnp.var(x, axis=axis, keepdims=True)
    return (x - m) / jnp.sqrt(v + eps)

def _scatter_add(tgt, idx, src, axis=0):
    return tgt.at[idx].add(src)

def _segment_sum(src, seg, n):
    return jax.ops.segment_sum(src, seg, n)
kernel_name = 'mk_adj_resnorm_d4_adj_r2_d4ac73'

def setup_inputs(seed: int=0):
    np.random.seed(seed)
    _w = jnp.asarray

    def _rec_inputs():
        import jax
        import jax.numpy as jnp
        _gk = jax.random.key(seed)
        x = -0.001547 + 1.001 * jax.random.normal(jax.random.fold_in(_gk, 1), (64, 128, 128), jnp.float32)
        _a = jax.random.bernoulli(jax.random.fold_in(_gk, 2), 0.03125, (64, 128, 128))
        _a = jnp.logical_or(_a, jnp.swapaxes(_a, -1, -2))
        _a = jnp.logical_or(_a, jnp.eye(128, dtype=bool))
        _af = _a.astype(jnp.float32)
        _af = _af * jax.random.uniform(jax.random.fold_in(_gk, 3), (64, 128, 128), jnp.float32, 0.05, 4.99997)
        adj = _af
        _nm = jnp.ones((64, 128), dtype=bool)
        nodemask = jnp.where(_nm, 1.0, 0.0).astype(jnp.float32)
        return (x, adj, nodemask)
    x, adj, nodemask = _rec_inputs()

    def _L0_gnn_setup():
        import jax, jax.numpy as jnp
        import numpy as np
        B, N, NAB, NF, NG = (8, 128, 128, 128, 64)
        CUTOFF = 5.0
        LN2 = float(np.log(2.0))

        def ssp(x):
            return jax.nn.softplus(x) - LN2
        key = jax.random.key(seed)
        ks = jax.random.split(key, 12)
        r = jax.random.normal(ks[0], (B, N, NAB), dtype=jnp.float32)
        e = jax.random.uniform(ks[1], (B, N, N), dtype=jnp.float32) * CUTOFF
        A = (jax.random.uniform(ks[2], (B, N, N)) < 0.3).astype(jnp.float32)
        s = 0.05
        W1 = jax.random.normal(ks[3], (NF, NG), dtype=jnp.float32) * s
        b1 = jnp.zeros((NF,), jnp.float32)
        W2 = jax.random.normal(ks[4], (NF, NF), dtype=jnp.float32) * s
        b2 = jnp.zeros((NF,), jnp.float32)
        Wa = jax.random.normal(ks[5], (NF, NAB), dtype=jnp.float32) * s
        Wd1 = jax.random.normal(ks[6], (NAB, NF), dtype=jnp.float32) * s
        bd1 = jnp.zeros((NAB,), jnp.float32)
        Wd2 = jax.random.normal(ks[7], (NAB, NAB), dtype=jnp.float32) * s
        bd2 = jnp.zeros((NAB,), jnp.float32)
        return {'r': r, 'e': e, 'A': A, 'W1': W1, 'b1': b1, 'W2': W2, 'b2': b2, 'Wa': Wa, 'Wd1': Wd1, 'bd1': bd1, 'Wd2': Wd2, 'bd2': bd2}
    _L0_gnn_all = _L0_gnn_setup()
    _L0_gnn_in = {k: v for k, v in _L0_gnn_all.items() if k in ('W1', 'b1', 'W2', 'b2', 'Wa', 'Wd1', 'bd1', 'Wd2', 'bd2')}
    del _L0_gnn_all

    def _L1_gnn_setup():
        import jax, jax.numpy as jnp
        import numpy as np
        B, A, H = (8, 1024, 128)
        D = 128
        TOPK = 8
        SCALE = float(np.sqrt(D))
        LN_EPS = 1e-05
        key = jax.random.key(seed)
        ks = jax.random.split(key, 5)
        x = jax.random.normal(ks[0], (B, A, H), dtype=jnp.float32)
        connectivity = jax.random.normal(ks[1], (B, A, A), dtype=jnp.float32)
        Wq = jax.random.normal(ks[2], (H, D), dtype=jnp.float32) / np.sqrt(H)
        Wk = jax.random.normal(ks[3], (H, D), dtype=jnp.float32) / np.sqrt(H)
        Wv = jax.random.normal(ks[4], (H, D), dtype=jnp.float32) / np.sqrt(H)
        gamma = jnp.ones((D,), dtype=jnp.float32)
        beta = jnp.zeros((D,), dtype=jnp.float32)
        return {'x': x, 'connectivity': connectivity, 'Wq': Wq, 'Wk': Wk, 'Wv': Wv, 'gamma': gamma, 'beta': beta}
    _L1_gnn_all = _L1_gnn_setup()
    _L1_gnn_in = {k: v for k, v in _L1_gnn_all.items() if k in ('Wq', 'Wk', 'Wv', 'gamma', 'beta')}
    del _L1_gnn_all

    def _L2_gnn_setup():
        import jax, jax.numpy as jnp
        import numpy as np
        B, N, F, H = (32, 512, 128, 128)
        NEG_BIG = -10000000000.0
        if __name__ == '__main__':
            out = reference(**setup_inputs())
            print(out.shape, out.dtype)
        key = jax.random.key(seed)
        ks = jax.random.split(key, 8)
        M_features = jax.random.normal(ks[0], (B, N, F), dtype=jnp.float32)
        adj = (jax.random.uniform(ks[1], (B, N, N)) < 0.05).astype(jnp.float32)
        eye = jnp.eye(N, dtype=jnp.float32)[None]
        M_adjacency = jnp.maximum(adj, eye)
        mask = (jnp.arange(N)[None, :] < 3 * N // 4).astype(jnp.float32)
        mask = jnp.broadcast_to(mask, (B, N)).astype(jnp.float32)
        he = lambda k, shp: jax.random.normal(k, shp, jnp.float32) * np.sqrt(2.0 / shp[0])
        W_layer = he(ks[2], (F, H))
        b_layer = jnp.zeros((H,), jnp.float32)
        W_att_self = he(ks[3], (H, 1))
        W_att_neighbor = he(ks[4], (H, 1))
        return {'M_features': M_features, 'M_adjacency': M_adjacency, 'mask': mask, 'W_layer': W_layer, 'b_layer': b_layer, 'W_att_self': W_att_self, 'W_att_neighbor': W_att_neighbor}
    _L2_gnn_all = _L2_gnn_setup()
    _L2_gnn_in = {k: v for k, v in _L2_gnn_all.items() if k in ('W_layer', 'b_layer', 'W_att_self', 'W_att_neighbor')}
    del _L2_gnn_all

    def _L3_gnn_setup():
        import jax, jax.numpy as jnp
        import numpy as np
        HID = 128

        def preprocess_adj(A):
            N = A.shape[1]
            A_hat = A + jnp.eye(N, dtype=A.dtype)
            d = jnp.sum(A_hat, axis=2)
            d_safe = jnp.where(d > 0, d, 1.0)
            d_inv = jnp.where(d > 0, d_safe ** (-0.5), 0.0)
            return d_inv[:, :, None] * A_hat * d_inv[:, None, :]

        def lstm(x, w_ih, w_hh, b_ih, b_hh):
            B = x.shape[0]
            H = w_hh.shape[1]

            def step(carry, xt):
                h, c = carry
                z = xt @ w_ih.T + b_ih + h @ w_hh.T + b_hh
                i, f, g, o = jnp.split(z, 4, axis=-1)
                c = jax.nn.sigmoid(f) * c + jax.nn.sigmoid(i) * jnp.tanh(g)
                h = jax.nn.sigmoid(o) * jnp.tanh(c)
                return ((h, c), h)
            h0 = jnp.zeros((B, H), x.dtype)
            c0 = jnp.zeros((B, H), x.dtype)
            _, hs = jax.lax.scan(step, (h0, c0), jnp.swapaxes(x, 0, 1))
            return jnp.swapaxes(hs, 0, 1)

        def gcn_dynamic_forward(x, A_norm, conv_w, conv_b, w_ih, w_hh, b_ih, b_hh):
            df_in = x[:, x.shape[1] - HID:, :]
            dyn = jax.lax.conv_general_dilated(df_in, conv_w, window_strides=(1,), padding=[(1, 1)], dimension_numbers=('NCH', 'OIH', 'NCH')) + conv_b[None, :, None]
            lw = lstm(dyn, w_ih, w_hh, b_ih, b_hh)
            agg = jnp.matmul(A_norm, x)
            out = jax.nn.sigmoid(jnp.matmul(agg, lw))
            return out
        key = jax.random.key(seed)
        ks = jax.random.split(key, 8)
        B, N = (4, 2048)
        node_embedding = jax.random.normal(ks[0], (B, N, HID), dtype=jnp.float32)
        adjacency_matrix = (jax.random.uniform(ks[1], (B, N, N)) < 0.01).astype(jnp.float32)
        s = 0.05
        conv_w = jax.random.normal(ks[2], (HID, HID, 3), dtype=jnp.float32) * s
        conv_b = jax.random.normal(ks[3], (HID,), dtype=jnp.float32) * s
        w_ih = jax.random.normal(ks[4], (4 * HID, HID), dtype=jnp.float32) * s
        w_hh = jax.random.normal(ks[5], (4 * HID, HID), dtype=jnp.float32) * s
        b_ih = jax.random.normal(ks[6], (4 * HID,), dtype=jnp.float32) * s
        b_hh = jax.random.normal(ks[7], (4 * HID,), dtype=jnp.float32) * s
        return {'node_embedding': node_embedding, 'adjacency_matrix': adjacency_matrix, 'conv_w': conv_w, 'conv_b': conv_b, 'w_ih': w_ih, 'w_hh': w_hh, 'b_ih': b_ih, 'b_hh': b_hh}
    _L3_gnn_all = _L3_gnn_setup()
    _L3_gnn_in = {k: v for k, v in _L3_gnn_all.items() if k in ('conv_w', 'conv_b', 'w_ih', 'w_hh', 'b_ih', 'b_hh')}
    del _L3_gnn_all
    return {'x': x, 'adj': adj, 'nodemask': nodemask, 'L0_gnn_W1': _L0_gnn_in['W1'], 'L0_gnn_b1': _L0_gnn_in['b1'], 'L0_gnn_W2': _L0_gnn_in['W2'], 'L0_gnn_b2': _L0_gnn_in['b2'], 'L0_gnn_Wa': _L0_gnn_in['Wa'], 'L0_gnn_Wd1': _L0_gnn_in['Wd1'], 'L0_gnn_bd1': _L0_gnn_in['bd1'], 'L0_gnn_Wd2': _L0_gnn_in['Wd2'], 'L0_gnn_bd2': _L0_gnn_in['bd2'], 'L1_gnn_Wq': _L1_gnn_in['Wq'], 'L1_gnn_Wk': _L1_gnn_in['Wk'], 'L1_gnn_Wv': _L1_gnn_in['Wv'], 'L1_gnn_gamma': _L1_gnn_in['gamma'], 'L1_gnn_beta': _L1_gnn_in['beta'], 'L2_gnn_W_layer': _L2_gnn_in['W_layer'], 'L2_gnn_b_layer': _L2_gnn_in['b_layer'], 'L2_gnn_W_att_self': _L2_gnn_in['W_att_self'], 'L2_gnn_W_att_neighbor': _L2_gnn_in['W_att_neighbor'], 'L3_gnn_conv_w': _L3_gnn_in['conv_w'], 'L3_gnn_conv_b': _L3_gnn_in['conv_b'], 'L3_gnn_w_ih': _L3_gnn_in['w_ih'], 'L3_gnn_w_hh': _L3_gnn_in['w_hh'], 'L3_gnn_b_ih': _L3_gnn_in['b_ih'], 'L3_gnn_b_hh': _L3_gnn_in['b_hh']}

def reference(x, adj, nodemask, L0_gnn_W1, L0_gnn_b1, L0_gnn_W2, L0_gnn_b2, L0_gnn_Wa, L0_gnn_Wd1, L0_gnn_bd1, L0_gnn_Wd2, L0_gnn_bd2, L1_gnn_Wq, L1_gnn_Wk, L1_gnn_Wv, L1_gnn_gamma, L1_gnn_beta, L2_gnn_W_layer, L2_gnn_b_layer, L2_gnn_W_att_self, L2_gnn_W_att_neighbor, L3_gnn_conv_w, L3_gnn_conv_b, L3_gnn_w_ih, L3_gnn_w_hh, L3_gnn_b_ih, L3_gnn_b_hh):
    import jax
    import jax.numpy as jnp

    def _L0_gnn_ref(r, e, A, W1, b1, W2, b2, Wa, Wd1, bd1, Wd2, bd2):
        import jax, jax.numpy as jnp
        import numpy as np
        B, N, NAB, NF, NG = (8, 128, 128, 128, 64)
        CUTOFF = 5.0
        LN2 = float(np.log(2.0))

        def ssp(x):
            return jax.nn.softplus(x) - LN2
        offsets = jnp.linspace(0.0, CUTOFF, NG, dtype=jnp.float32)
        width = offsets[1] - offsets[0]
        coeff = -0.5 / (width * width)
        diff = e[:, :, :, None] - offsets
        g = jnp.exp(coeff * diff * diff)
        h = ssp(jnp.einsum('bijg,fg->bijf', g, W1) + b1)
        Wf = jnp.einsum('bijf,gf->bijg', h, W2) + b2
        rf = jnp.einsum('bjd,fd->bjf', r, Wa)
        Am = A[:, :, :, None]
        Wf = Wf * Am
        y = jnp.einsum('bjf,bijf->bif', rf, Wf * Am)
        y = ssp(jnp.einsum('bif,df->bid', y, Wd1) + bd1)
        y = jnp.einsum('bid,ed->bie', y, Wd2) + bd2
        return y

    def _L1_gnn_ref(x, connectivity, Wq, Wk, Wv, gamma, beta):
        import jax, jax.numpy as jnp
        import numpy as np
        B, A, H = (8, 1024, 128)
        D = 128
        TOPK = 8
        SCALE = float(np.sqrt(D))
        LN_EPS = 1e-05
        Q = jnp.einsum('bah,hd->bad', x, Wq)
        K = jnp.einsum('bah,hd->bad', x, Wk)
        V = jnp.einsum('bah,hd->bad', x, Wv)
        scores = jnp.einsum('bad,bcd->bac', Q, K) / SCALE + connectivity
        topk_vals, topk_idx = jax.lax.top_k(scores, TOPK)
        probs = jax.nn.softmax(topk_vals, axis=-1)
        Vg = jax.vmap(lambda v, i: v[i])(V, topk_idx)
        out = jnp.einsum('bak,bakd->bad', probs, Vg)
        mu = jnp.mean(out, axis=-1, keepdims=True)
        var = jnp.mean(jnp.square(out - mu), axis=-1, keepdims=True)
        return (out - mu) * jax.lax.rsqrt(var + LN_EPS) * gamma + beta

    def _L2_gnn_ref(M_features, M_adjacency, mask, W_layer, b_layer, W_att_self, W_att_neighbor):
        import jax, jax.numpy as jnp
        import numpy as np
        B, N, F, H = (32, 512, 128, 128)
        NEG_BIG = -10000000000.0
        if __name__ == '__main__':
            out = reference(**setup_inputs())
            print(out.shape, out.dtype)
        h = jnp.einsum('bnf,fh->bnh', M_features, W_layer)
        a_self = jnp.einsum('bnh,ho->bno', h, W_att_self)
        a_neigh = jnp.einsum('bnh,ho->bno', h, W_att_neighbor)
        logits = a_self + jnp.transpose(a_neigh, (0, 2, 1))
        logits = jax.nn.leaky_relu(logits, negative_slope=0.2)
        logits = logits + NEG_BIG * (1.0 - M_adjacency)
        attention = jax.nn.softmax(logits, axis=-1)
        h_prime = jnp.einsum('bnm,bmh->bnh', attention, h) + b_layer[None, None, :]
        h_prime = h_prime * mask[:, :, None]
        return h_prime

    def _L3_gnn_ref(node_embedding, adjacency_matrix, conv_w, conv_b, w_ih, w_hh, b_ih, b_hh):
        import jax, jax.numpy as jnp
        import numpy as np
        HID = 128

        def preprocess_adj(A):
            N = A.shape[1]
            A_hat = A + jnp.eye(N, dtype=A.dtype)
            d = jnp.sum(A_hat, axis=2)
            d_safe = jnp.where(d > 0, d, 1.0)
            d_inv = jnp.where(d > 0, d_safe ** (-0.5), 0.0)
            return d_inv[:, :, None] * A_hat * d_inv[:, None, :]

        def lstm(x, w_ih, w_hh, b_ih, b_hh):
            B = x.shape[0]
            H = w_hh.shape[1]

            def step(carry, xt):
                h, c = carry
                z = xt @ w_ih.T + b_ih + h @ w_hh.T + b_hh
                i, f, g, o = jnp.split(z, 4, axis=-1)
                c = jax.nn.sigmoid(f) * c + jax.nn.sigmoid(i) * jnp.tanh(g)
                h = jax.nn.sigmoid(o) * jnp.tanh(c)
                return ((h, c), h)
            h0 = jnp.zeros((B, H), x.dtype)
            c0 = jnp.zeros((B, H), x.dtype)
            _, hs = jax.lax.scan(step, (h0, c0), jnp.swapaxes(x, 0, 1))
            return jnp.swapaxes(hs, 0, 1)

        def gcn_dynamic_forward(x, A_norm, conv_w, conv_b, w_ih, w_hh, b_ih, b_hh):
            df_in = x[:, x.shape[1] - HID:, :]
            dyn = jax.lax.conv_general_dilated(df_in, conv_w, window_strides=(1,), padding=[(1, 1)], dimension_numbers=('NCH', 'OIH', 'NCH')) + conv_b[None, :, None]
            lw = lstm(dyn, w_ih, w_hh, b_ih, b_hh)
            agg = jnp.matmul(A_norm, x)
            out = jax.nn.sigmoid(jnp.matmul(agg, lw))
            return out
        A_norm = preprocess_adj(adjacency_matrix)
        return gcn_dynamic_forward(node_embedding, A_norm, conv_w, conv_b, w_ih, w_hh, b_ih, b_hh)
    x = _layernorm(x + _L0_gnn_ref(x, adj, adj, L0_gnn_W1, L0_gnn_b1, L0_gnn_W2, L0_gnn_b2, L0_gnn_Wa, L0_gnn_Wd1, L0_gnn_bd1, L0_gnn_Wd2, L0_gnn_bd2), axis=-1)
    x = _layernorm(x + _L1_gnn_ref(x, adj, L1_gnn_Wq, L1_gnn_Wk, L1_gnn_Wv, L1_gnn_gamma, L1_gnn_beta), axis=-1)
    x = _layernorm(x + _L2_gnn_ref(x, adj, nodemask, L2_gnn_W_layer, L2_gnn_b_layer, L2_gnn_W_att_self, L2_gnn_W_att_neighbor), axis=-1)
    x = _layernorm(x + _L3_gnn_ref(x, adj, L3_gnn_conv_w, L3_gnn_conv_b, L3_gnn_w_ih, L3_gnn_w_hh, L3_gnn_b_ih, L3_gnn_b_hh), axis=-1)
    return x

_drawn_inputs = setup_inputs


def setup_inputs(seed=0):
    import zlib

    import numpy as np

    out = dict(_drawn_inputs(seed))
    spreads = {'L0_gnn_b1': (0.0, 0.1),
     'L0_gnn_b2': (0.0, 0.1),
     'L0_gnn_bd1': (0.0, 0.1),
     'L0_gnn_bd2': (0.0, 0.1),
     'L1_gnn_gamma': (1.0, 0.2),
     'L1_gnn_beta': (0.0, 0.1),
     'L2_gnn_b_layer': (0.0, 0.1)}
    factors = {'L3_gnn_conv_b': 6.787, 'L3_gnn_b_ih': 5.689, 'L3_gnn_b_hh': 5.716}
    for name, (base, spread) in spreads.items():
        noise = np.random.default_rng([zlib.crc32(name.encode()), seed]).standard_normal(out[name].shape)
        drawn = base * np.exp(spread * noise) if base else spread * noise
        out[name] = jnp.asarray(drawn.astype(out[name].dtype))
    for name, factor in factors.items():
        out[name] = (out[name] * factor).astype(out[name].dtype)
    return out
```

```python
from contextlib import ExitStack

import numpy as np
import concourse.bass as bass
from concourse import mybir

ALU = mybir.AluOpType
ACT = mybir.ActivationFunctionType
AX = mybir.AxisListType
F32 = mybir.dt.float32
BF16 = mybir.dt.bfloat16
U32 = mybir.dt.uint32
I32 = mybir.dt.int32

P = 128
B = 64
NG = 64
CUTOFF = 5.0
R = 6
UNIT = R * P
HALF = UNIT // 2
DIRECT = 2 * R - 1
RANKS = 24
OVER = RANKS - DIRECT
ALL_UNITS = -(-P // R)
UNIT_BUFS = 4
CLAMP = 40.0
LN2 = float(np.log(2.0))
EPS = 1e-5
G = 4


def gaussian_constants():
    offsets = np.linspace(0.0, CUTOFF, NG, dtype=np.float32)
    width = np.float32(offsets[1] - offsets[0])
    return offsets, float(np.float32(-0.5) / (width * width))


class Steps:

    def __init__(self, pair, inner, per_pair, total):
        self.pair, self.inner, self.per_pair, self.total = pair, inner, per_pair, total
        self.static = isinstance(pair, int)

    def has(self, d=0):
        return not self.static or 0 <= self.pair * self.per_pair + self.inner + d < self.total

    def at(self, d=0):
        return self.pair * self.per_pair + (self.inner + d)

    def mod(self, n, d=0):
        return (self.inner + d) % n


def pairs(eng, first, loop, last, body):
    for pair in first:
        body(pair)
    with eng.Fori(loop[0], loop[1]) as pair:
        body(pair)
    for pair in last:
        body(pair)


def build(nc, a, out):
    offsets, coeff = gaussian_constants()
    ctx = ExitStack()
    with ctx:
        def sb(name, shape, dt=F32):
            return ctx.enter_context(nc.sbuf_tensor(name, shape, dt))

        xin = sb("xin", [P, B, P])
        xres = sb("xres", [P, B, P])
        ident = sb("ident", [P, P])
        iota_row = sb("iota_row", [P, P])
        iota_col = sb("iota_col", [P, 1])
        flag = sb("flag", [1, 1], I32)
        deg = sb("deg", [P, 2, G])
        edge_val = nc.dram_tensor("edge_val", [B, 2, P, R], F32, kind="Internal").ap()
        edge_idx = nc.dram_tensor("edge_idx", [B, 2, P, R], BF16, kind="Internal").ap()
        all_idx = nc.dram_tensor("all_idx", [ALL_UNITS, P * R], BF16, kind="Internal").ap()

        held = {n: ctx.enter_context(nc.semaphore("held_" + n)) for n in ("SP", "DVE", "Pool")}

        k = dict(locals())
        k["phase_semaphores"] = []
        constants_block(nc, k)
        with ExitStack() as c0:
            k["c0"] = c0
            layer0(nc, a, k)
            clear_semaphores(nc, k)
        k["dyn"] = sb("dyn", [P, P, B])
        k["agg"] = sb("agg", [P, B, P])
        k["dinv"] = sb("dinv", [P, B])
        layers12(nc, a, k)
        lstm(nc, a, k)


def phase_semaphore(nc, stack, k, name):
    handle = stack.enter_context(nc.semaphore(name))
    k["phase_semaphores"].append(handle)
    return handle


def clear_semaphores(nc, k):
    with ExitStack() as c:
        block = c.enter_context(nc.Block())

        @block.sync
        def _(sp):
            for handle in k["phase_semaphores"]:
                sp.sem_clear(handle)
    k["phase_semaphores"].clear()


def constants_block(nc, k):
    with ExitStack() as c:
        iota_done, cast_done, all_idx_stored = (k["ctx"].enter_context(nc.semaphore(n))
                                                for n in ("iota_done", "cast_done", "all_idx_stored"))
        columns = c.enter_context(nc.sbuf_tensor("columns", [ALL_UNITS, P * R], F32))
        columns16 = c.enter_context(nc.sbuf_tensor("columns16", [ALL_UNITS, P * R], BF16))
        block = c.enter_context(nc.Block())

        @block.gpsimd
        def _(pool):
            pool.iota(k["iota_row"][:, :], pattern=[[1, P]], base=0, channel_multiplier=0,
                      allow_small_or_imprecise_dtypes=True).then_inc(iota_done, 1)
            pool.iota(k["iota_col"][:, :], pattern=[[0, 1]], base=0, channel_multiplier=1,
                      allow_small_or_imprecise_dtypes=True).then_inc(iota_done, 1)
            pool.iota(columns[:, :].rearrange("u (i r) -> u i r", r=R), pattern=[[0, P], [1, R]], base=0,
                      channel_multiplier=R, allow_small_or_imprecise_dtypes=True).then_inc(iota_done, 1)

        @block.vector
        def _(dve):
            dve.wait_ge(iota_done, 2)
            dve.tensor_scalar(k["ident"][:, :], k["iota_row"][:, :], k["iota_col"][:, :], None, ALU.is_equal)
            dve.wait_ge(iota_done, 3)
            dve.tensor_copy(columns16[:, :], columns[:, :]).then_inc(cast_done, 1)

        @block.sync
        def _(sp):
            sp.wait_ge(cast_done, 1)
            sp.dma_start(k["all_idx"], columns16[:, :]).then_inc(all_idx_stored, 16)
            sp.wait_ge(all_idx_stored, 16)


def layer0(nc, a, k):
    c0 = k["c0"]
    offsets, coeff = gaussian_constants()
    xin, xres, ident, iota_row, iota_col, flag = (k[n] for n in ("xin", "xres", "ident", "iota_row", "iota_col", "flag"))
    edge_val, edge_idx = k["edge_val"], k["edge_idx"]

    def sb(name, shape, dt=F32):
        return c0.enter_context(nc.sbuf_tensor(name, shape, dt))

    def ps(name, shape, dt=F32):
        return c0.enter_context(nc.psum_tensor(name, shape, dt))

    def sem(name):
        return phase_semaphore(nc, c0, k, name)

    w1t = sb("w1t", [P, P])
    w2t = sb("w2t", [P, P])
    wat = sb("wat", [P, P])
    wd1t = sb("wd1t", [P, P])
    wd2t = sb("wd2t", [P, P])
    b1c = sb("b1c", [P, 1])
    bd1c = sb("bd1c", [P, 1])
    off_c = sb("off_c", [P, 1])
    noff_c = sb("noff_c", [P, 1])
    b2row = sb("b2row", [1, P])
    bd2row = sb("bd2row", [1, P])
    ones_row = sb("ones_row", [1, P])
    mln2 = sb("mln2", [P, P])
    before = sb("before", [P, P])
    b2bc = sb("b2bc", [P, P])
    bd2bc = sb("bd2bc", [P, P])
    adj_w = sb("adj_w", [P, 2, P])
    adj_r1 = sb("adj_r1", [P, P])
    adj_r2 = sb("adj_r2", [P, P])
    found = sb("found", [P, 2 * RANKS + 2])
    found_idx = sb("found_idx", [P, RANKS], U32)
    over_bits = sb("over_bits", [P, OVER])
    over_cnt = sb("over_cnt", [P, 1])
    slot_from = sb("slot_from", [P, P])
    slot_of = sb("slot_of", [P, P])
    rank_hit = sb("rank_hit", [P, OVER])
    over_pick = sb("over_pick", [P, 2, OVER])
    ev = sb("ev", [P, 2, 2 * R])
    ei = sb("ei", [P, 2, 2 * R])
    ei16 = sb("ei16", [P, 2, 2 * R], BF16)
    over_row = sb("over_row", [P, B])
    over_end = sb("over_end", [P, B])
    last_rank = sb("last_rank", [P, B])
    least = sb("least", [P, B])
    over_t = sb("over_t", [P, 2, P])
    val_bc = sb("val_bc", [P, UNIT_BUFS, HALF])
    idx_bc = sb("idx_bc", [P, UNIT_BUFS, UNIT], BF16)
    val_own = sb("val_own", [P, UNIT_BUFS, R])
    val_sq = sb("val_sq", [P, UNIT_BUFS, R])
    dist2 = sb("dist2", [P, HALF])
    gauss = sb("gauss", [P, 2, HALF])
    pick = sb("pick", [P, 2, UNIT], BF16)
    clamped = sb("clamped", [P, UNIT])
    expd = sb("expd", [P, UNIT])
    logd = sb("logd", [P, UNIT])
    hid = sb("hid", [P, 2, UNIT])
    rfe = sb("rfe", [P, 2, UNIT])
    msg = sb("msg", [P, 2, UNIT])
    xt_w = sb("xt_w", [P, 2, P])
    adjt_w = sb("adjt_w", [P, 2, P])
    adjt_sq = sb("adjt_sq", [P, 2, P])
    rf_hi = sb("rf_hi", [P, 2, P], BF16)
    rf_mid = sb("rf_mid", [P, 2, P], BF16)
    rf_lo = sb("rf_lo", [P, 2, P], BF16)
    rf_r1 = sb("rf_r1", [P, P])
    rfb = sb("rfb", [P, 2, P])
    xb = sb("xb", [P, 2, P])
    yt = sb("yt", [P, P])
    t_u = sb("t_u", [P, P])
    t_cl = sb("t_cl", [P, P])
    t_ex = sb("t_ex", [P, P])
    t_lg = sb("t_lg", [P, P])
    t_h = sb("t_h", [P, P])
    v0 = sb("v0", [P, 4])

    zb = ps("zb", [P, 2, 512])
    wf = ps("wf", [P, 2, 512])
    rg = ps("rg", [P, 2, 512])
    yp = ps("yp", [P, 512])
    mb = ps("mb", [P, 512])
    p_out = rg[:, 0, HALF:512]
    p_u = rg[:, 1, HALF:512]
    p_rf = mb[:, 0:P]
    p_over = mb[:, P:P + 2 * RANKS + 2]
    p_start = mb[:, 200:201]
    p_flag = mb[0:1, 201:202]

    def column(bank_pair, r):
        return bank_pair[:, r // 3, r % 3 * P:(r % 3 + 1) * P]

    weights_in = sem("weights_in")
    x_in = sem("x_in")
    adj_in = [sem(f"adj_in{i}") for i in range(2)]
    xt_in = [sem(f"xt_in{i}") for i in range(2)]
    adjt_in = [sem(f"adjt_in{i}") for i in range(2)]
    edges_stored = sem("edges_stored")
    unit_in = [sem(f"unit_in{i}") for i in range(UNIT_BUFS)]
    names = (
        "consts_ready bias_ready bias_read memsets_done "
        "top1 top2 top3 rest1 rest2 idx3 idxf cnt start_ready start_copied from_ready slot_ready over_gathered "
        "hits_ready picks_ready edges16 adj_read "
        "dist2_ready gauss_ready z_ready clamped_ready exp_ready log_ready hid_ready pick_ready valsq_ready "
        "rg_ready rfe_ready wf_ready msg_ready summed "
        "rf_ready rfhi_ready rfr1_ready rfmid_ready rflo_ready rfb_ready adjtsq_ready xb_ready yt_ready u_ready "
        "u_read uclamped_ready uexp_ready ulog_ready uh_ready out_ready res_ready over_t_ready"
    ).split()
    s = {n: sem("l0_" + n) for n in names}

    n_weights = 12

    with ExitStack() as c1:
        block = c1.enter_context(nc.Block())

        @block.sync
        def _(sp):
            for half in range(2):
                sp.dma_start(w1t[half * NG:(half + 1) * NG, :], a["w1t"]).then_inc(weights_in, 16)
                sp.dma_start(off_c[half * NG:(half + 1) * NG, :], a["offsets"]).then_inc(weights_in, 16)
            for dst, src in ((w2t, "w2t"), (wat, "wat"), (wd1t, "wd1t"), (wd2t, "wd2t"), (b1c, "b1c"),
                             (bd1c, "bd1c"), (b2row, "b2row"), (bd2row, "bd2row")):
                sp.dma_start(dst[:, :], a[src]).then_inc(weights_in, 16)

        @block.vector
        def _(dve):
            dve.memset(mln2[:, :], -LN2)
            dve.memset(ones_row[:, :], 1.0)
            dve.memset(over_row[:, :], 0.0)
            dve.tensor_scalar(before[:, :], iota_row[:, :], iota_col[:, :], None, ALU.is_gt)
            dve.tensor_copy(found[:, 2 * RANKS + 1:], iota_col[:, :]).then_inc(s["consts_ready"], 1)
            dve.wait_ge(weights_in, 16 * n_weights)
            dve.tensor_scalar(noff_c[:, :], off_c[:, :], -1.0, None, ALU.mult)
            dve.wait_ge(s["bias_ready"], 1)
            dve.tensor_copy(b2bc[:, :], p_rf)
            dve.tensor_copy(bd2bc[:, :], p_u)

        @block.tensor
        def _(pe):
            pe.wait_ge(weights_in, 16 * n_weights)
            pe.wait_ge(s["consts_ready"], 1)
            pe.matmul(p_rf, mln2[:, :], w2t[:, :], start=True, stop=False)
            pe.matmul(p_rf, ones_row[:, :], b2row[:, :], start=False, stop=True)
            pe.matmul(p_u, mln2[:, :], wd2t[:, :], start=True, stop=False)
            pe.matmul(p_u, ones_row[:, :], bd2row[:, :], start=False, stop=True).then_inc(s["bias_ready"], 1)

    def run(block, dense):
        per_graph = ALL_UNITS if dense else 2
        per_pair = 2 * per_graph
        nu, ng = per_graph * B, B
        u0 = 2 * B if dense else 0
        g0 = B if dense else 0
        val_src = a["adj_cols"] if dense else edge_val
        idx_src = k["all_idx"] if dense else edge_idx
        buf_base = 0

        def unit(pair, i):
            return Steps(pair, i, per_pair, nu)

        def graph(pair, i):
            return Steps(pair, i // per_graph, 2, ng)

        def unit_count(u, d, q):
            before_pair = per_pair // UNIT_BUFS
            return u.pair * (64 * before_pair) + 64 * ((u.inner + d) // UNIT_BUFS + 1 + u0 // UNIT_BUFS)

        def adj_count(g, q, d=0):
            return g.pair * 16 + 16 * ((g.inner + d) // 2 + 1 + g0 // 2)

        def schedule(eng, body):
            if dense:
                pairs(eng, (-1, 0), (1, B // 2 - 1), (B // 2 - 1, B // 2), body)
            else:
                pairs(eng, (-2, -1, 0), (1, B // 2 - 2), (B // 2 - 2, B // 2 - 1, B // 2), body)

        def w(eng, name, value):
            eng.wait_ge(s[name], value)

        def after(eng, name, st, d, start):
            i = min(st.at(d), st.total - 1) if st.static else st.at(d)
            if not st.static or i + start >= 0:
                eng.wait_ge(s[name], i + start + 1)

        def after_graph(eng, g, d, name="summed"):
            if not g.static or g.at(d) + g0 >= 0:
                eng.wait_ge(s[name], (g.at(d) + 1) * per_graph + u0 if not g.static or g.at(d) >= 0
                            else 2 * (g.at(d) + g0 + 1))

        def alone(eng):
            eng.sem_inc(k["held"][eng.engine.name], 1)

        @block.sync
        def _(sp):
            if not dense:
                for c in range(4):
                    sp.dma_start(xin[:, c * (B // 4):(c + 1) * (B // 4), :],
                                 a["x_rows"][:, c * (B // 4):(c + 1) * (B // 4), :]).then_inc(x_in, 16)

            def load_unit(u, d, g, dg, kk):
                q = u.mod(UNIT_BUFS, d)
                after(sp, "dist2_ready", u, d - UNIT_BUFS, u0)
                after(sp, "pick_ready", u, d - UNIT_BUFS, u0)
                after(sp, "valsq_ready", u, d - UNIT_BUFS, u0)
                alone(sp)
                lo, hi = slice(0, NG), slice(NG, P)
                gi = g.at(dg)
                for half, part in ((0, lo), (1, hi)):
                    sp.dma_start(val_bc[part, q, :],
                                 val_src[bass.ds(gi, 1), kk, half * NG:(half + 1) * NG, :]
                                 .rearrange("a i r -> a (i r)").broadcast_to((NG, HALF))).then_inc(unit_in[q], 16)
                if dense:
                    isrc = idx_src[kk:kk + 1, :].broadcast_to((P, UNIT))
                else:
                    isrc = idx_src[bass.ds(gi, 1), kk, :, :].rearrange("a i r -> a (i r)").broadcast_to((P, UNIT))
                sp.dma_start(idx_bc[:, q, :], isrc).then_inc(unit_in[q], 16)
                sp.dma_start(val_own[:, q, :],
                             val_src[bass.ds(gi, 1), kk, :, :].rearrange("a i r -> (a i) r")).then_inc(unit_in[q], 16)

            def body(pair):
                for i in range(per_pair):
                    u, g = unit(pair, i), graph(pair, i)
                    if i % per_graph == 0:
                        if not dense and g.has(4):
                            after(sp, "adj_read", g, 2, 0)
                            alone(sp)
                            sp.dma_start(adj_w[:, g.mod(2, 4), :], a["adj_rows"][:, g.at(4), :])\
                                .then_inc(adj_in[g.mod(2, 4)], 16)
                        if g.has(2):
                            after(sp, "rf_ready", g, 0, g0)
                            alone(sp)
                            sp.dma_start(xt_w[:, g.mod(2, 2), :], a["x_cols"][:, g.at(2), :])\
                                .then_inc(xt_in[g.mod(2, 2)], 16)
                        if g.has(1):
                            after(sp, "adjtsq_ready", g, -1, g0)
                            alone(sp)
                            sp.dma_start(adjt_w[:, g.mod(2, 1), :], a["adj_t"][:, g.at(1), :])\
                                .then_inc(adjt_in[g.mod(2, 1)], 16)
                    if not dense and i % 2 == 0 and g.has(2):
                        w(sp, "edges16", g.at(2) + 1)
                        alone(sp)
                        q = g.mod(2, 2)
                        sp.dma_start(edge_val[bass.ds(g.at(2), 1), :, :, :].rearrange("a h i r -> (a i) h r"),
                                     ev[:, q, :].rearrange("p (h r) -> p h r", h=2)).then_inc(edges_stored, 16)
                        sp.dma_start(edge_idx[bass.ds(g.at(2), 1), :, :, :].rearrange("a h i r -> (a i) h r"),
                                     ei16[:, q, :].rearrange("p (h r) -> p h r", h=2)).then_inc(edges_stored, 16)
                        sp.wait_ge(edges_stored, 32 * (g.at(2) + 1))
                        alone(sp)
                        for kk in range(2):
                            load_unit(u, 4 + kk, g, 2, kk)
                    if dense and u.has(3):
                        kk = (i + 3) % per_graph
                        load_unit(u, 3, g, (i + 3) // per_graph - i // per_graph, kk)
            schedule(sp, body)
            if not dense:
                sp.wait_ge(x_in, 64)

        @block.gpsimd
        def _(pool):
            if not dense:
                pool.wait_ge(x_in, 64)

            def body(pair):
                for i in range(per_pair):
                    u, g = unit(pair, i), graph(pair, i)
                    if u.has(1):
                        q = u.mod(UNIT_BUFS, 1)
                        if dense:
                            pool.wait_ge(unit_in[q], unit_count(u, 1, q))
                        else:
                            pool.wait_ge(unit_in[q], unit_count(u, 1, q))
                        after(pool, "msg_ready", u, 1 - UNIT_BUFS, u0)
                        pool.tensor_tensor(val_sq[:, q, :], val_own[:, q, :], val_own[:, q, :], ALU.mult)\
                            .then_inc(s["valsq_ready"], 1)
                    if i % per_graph == 0 and g.has(0):
                        q = g.mod(2)
                        pool.wait_ge(adjt_in[q], adj_count(g, q))
                        after_graph(pool, g, -2)
                        pool.tensor_tensor(adjt_sq[:, q, :], adjt_w[:, q, :], adjt_w[:, q, :], ALU.mult)\
                            .then_inc(s["adjtsq_ready"], 1)
                        after(pool, "res_ready", g, -2, g0)
                        pool.tensor_tensor(xb[:, q, :], xin[:, g.at(), :], bd2bc[:, :], ALU.add)\
                            .then_inc(s["xb_ready"], 1)
            schedule(pool, body)

        @block.scalar
        def _(act):
            if not dense:
                act.preload_act_table_set("natural_log_exp_and_others")

            def body(pair):
                for i in range(per_pair):
                    u, g = unit(pair, i), graph(pair, i)
                    k_in = i % per_graph
                    if u.has(0):
                        q = u.mod(2)
                        w(act, "rg_ready", u.at() + u0 + 1)
                        after(act, "msg_ready", u, -2, u0)
                        act.activation(rfe[:, q, :].rearrange("p (a n) -> p a n", a=2), rg[:, :, 0:HALF], ACT.Copy).then_inc(s["rfe_ready"], 1)
                    if u.has(2):
                        q = u.mod(UNIT_BUFS, 2)
                        act.wait_ge(unit_in[q], unit_count(u, 2, q))
                        after(act, "gauss_ready", u, 1, u0)
                        act.activation(dist2[:, :], val_bc[:, q, :], ACT.Square, bias=noff_c[:, :])\
                            .then_inc(s["dist2_ready"], 1)
                        w(act, "dist2_ready", u.at(2) + u0 + 1)
                        after(act, "z_ready", u, 0, u0)
                        act.activation(gauss[:, u.mod(2, 2), :], dist2[:, :], ACT.Exp, scale=coeff)\
                            .then_inc(s["gauss_ready"], 1)
                    if k_in == 0 and g.has(1):
                        w(act, "rf_ready", g.at(1) + g0 + 1)
                        after_graph(act, g, -1, "rg_ready")
                        act.activation(rf_hi[:, g.mod(2, 1), :], p_rf, ACT.Copy).then_inc(s["rfhi_ready"], 1)
                    if k_in == 1 and g.has(-1):
                        after_graph(act, g, -1)
                        after(act, "u_ready", g, -2, g0)
                        act.activation(yt[:, :], yp[:, 0:P], ACT.Copy).then_inc(s["yt_ready"], 1)
                    if u.has(1):
                        w(act, "clamped_ready", u.at(1) + u0 + 1)
                        after(act, "log_ready", u, 0, u0)
                        act.activation(expd[:, :], clamped[:, :], ACT.Exp).then_inc(s["exp_ready"], 1)
                        w(act, "exp_ready", u.at(1) + u0 + 1)
                        after(act, "hid_ready", u, 0, u0)
                        act.activation(logd[:, :], expd[:, :], ACT.Ln, bias=1.0).then_inc(s["log_ready"], 1)
                    if k_in == 0 and g.has(-2):
                        w(act, "uclamped_ready", g.at(-2) + g0 + 1)
                        after(act, "ulog_ready", g, -3, g0)
                        act.activation(t_ex[:, :], t_cl[:, :], ACT.Exp).then_inc(s["uexp_ready"], 1)
                        w(act, "uexp_ready", g.at(-2) + g0 + 1)
                        after(act, "uh_ready", g, -3, g0)
                        act.activation(t_lg[:, :], t_ex[:, :], ACT.Ln, bias=1.0).then_inc(s["ulog_ready"], 1)
            schedule(act, body)

        @block.tensor
        def _(pe):
            def body(pair):
                for i in range(per_pair):
                    u, g = unit(pair, i), graph(pair, i)
                    k_in = i % per_graph
                    q = u.mod(2)
                    if u.has(1):
                        qn = u.mod(2, 1)
                        w(pe, "gauss_ready", u.at(1) + u0 + 1)
                        after(pe, "hid_ready", u, 0, u0)
                        pe.matmul(zb[:, 0, 0:HALF], w1t[0:NG, :], gauss[0:NG, qn, :], start=True, stop=True)
                        pe.matmul(zb[:, 1, 0:HALF], w1t[NG:P, :], gauss[NG:P, qn, :], start=True, stop=True)\
                            .then_inc(s["z_ready"], 1)
                    if k_in == 1 and g.has(-1):
                        w(pe, "yt_ready", g.at(-1) + g0 + 1)
                        after(pe, "rfe_ready", u, 0, u0)
                        pe.matmul(p_u, wd1t[:, :], yt[:, :], start=True, stop=True).then_inc(s["u_ready"], 1)
                    if k_in == 1 and g.has(-2):
                        w(pe, "uh_ready", g.at(-2) + g0 + 1)
                        after(pe, "rfe_ready", u, 0, u0)
                        pe.matmul(p_out, t_h[:, :], wd2t[:, :], start=True, stop=True).then_inc(s["out_ready"], 1)
                    if u.has(0):
                        w(pe, "hid_ready", u.at() + u0 + 1)
                        after(pe, "msg_ready", u, -1, u0)
                        h = hid[:, q, :].rearrange("p (i r) -> p r i", r=R)
                        for r in range(R):
                            last = pe.matmul(column(wf, r), h[:, r, :], w2t[:, :], start=True, stop=True)
                        last.then_inc(s["wf_ready"], 1)
                    if u.has(1):
                        gn, kn = Steps(g.pair, (i + 1) // per_graph, 2, ng), (i + 1) % per_graph
                        w(pe, "pick_ready", u.at(1) + u0 + 1)
                        after(pe, "rfe_ready", u, 0, u0)
                        if kn == 0:
                            w(pe, "rflo_ready", gn.at() + g0 + 1)
                        if k_in == 1 and g.has(-1):
                            w(pe, "u_read", g.at(-1) + g0 + 1)
                        if k_in == 1 and g.has(-2):
                            w(pe, "res_ready", g.at(-2) + g0 + 1)
                        picked = pick[:, u.mod(2, 1), :].rearrange("p (i r) -> p r i", r=R)
                        for r in range(R):
                            for part in (rf_hi, rf_mid, rf_lo):
                                last = pe.matmul(column(rg, r), picked[:, r, :], part[:, gn.mod(2), :],
                                                 start=part is rf_hi, stop=part is rf_lo)
                        last.then_inc(s["rg_ready"], 1)
                    if k_in == 0 and g.has(1):
                        qg = g.mod(2, 1)
                        pe.wait_ge(xt_in[qg], adj_count(g, qg, 1))
                        if not dense and g.has(2):
                            w(pe, "edges16", g.at(2) + 1)
                        after(pe, "rfb_ready", g, 0, g0)
                        pe.matmul(p_rf, xt_w[:, qg, :], wat[:, :], start=True, stop=True).then_inc(s["rf_ready"], 1)
                    if u.has(-1):
                        ql = u.mod(2, -1)
                        gl = g if k_in > 0 else Steps(g.pair, g.inner - 1, 2, ng)
                        y = yp[:, 0:P]
                        kl = (k_in - 1) % per_graph
                        if kl == 0:
                            w(pe, "rfb_ready", gl.at() + g0 + 1)
                            w(pe, "adjtsq_ready", gl.at() + g0 + 1)
                            after(pe, "yt_ready", gl, -1, g0)
                            pe.matmul(y, rfb[:, gl.mod(2), :], adjt_sq[:, gl.mod(2), :], start=True, stop=False)
                        w(pe, "msg_ready", u.at(-1) + u0 + 1)
                        final = kl == per_graph - 1
                        if final and not dense:
                            w(pe, "over_t_ready", gl.at() + 1)
                        for r in range(R):
                            rows = over_t[:, gl.mod(2), :] if (final and not dense and r == R - 1) else ident[:, :]
                            last = pe.matmul(y, msg[:, ql, r * P:(r + 1) * P], rows, start=False,
                                             stop=final and r == R - 1)
                        last.then_inc(s["summed"], 1)
                    if not dense and k_in == 0 and g.has(3):
                        w(pe, "cnt", g.at(3) + 1)
                        if g.has(1):
                            w(pe, "rfb_ready", g.at(1) + 1)
                        pe.matmul(p_start, before[:, :], over_cnt[:, :], start=True, stop=True)\
                            .then_inc(s["start_ready"], 1)
                    if not dense and k_in == 1 and g.has(3):
                        w(pe, "slot_ready", g.at(3) + 1)
                        w(pe, "start_copied", g.at(3) + 1)
                        pe.matmul(p_over, slot_of[:, :], found[:, :], start=True, stop=True)\
                            .then_inc(s["over_gathered"], 1)
            schedule(pe, body)

        @block.vector
        def _(dve):
            def rank_edges(g):
                q, n = g.mod(2, 3), g.at(3) + 1
                dve.wait_ge(adj_in[q], g.pair * 16 + 16 * ((g.inner + 3) // 2 + 1))
                if not (g.static and not g.has(2)):
                    w(dve, "over_gathered", n - 1)
                    w(dve, "edges16", n - 1)
                alone(dve)
                adj = adj_w[:, q, :]
                dve.max(found[:, 0:8], adj).then_inc(s["top1"], 1)
                dve.tensor_reduce(least[:, bass.ds(g.at(3), 1)], adj, AX.X, ALU.min)
                w(dve, "top1", n)
                alone(dve)
                dve.match_replace(adj_r1[:, :], found[:, 0:8], adj, 0.0).then_inc(s["rest1"], 1)
                dve.max_index(found_idx[:, 0:8], found[:, 0:8], adj).then_inc(s["adj_read"], 1)
                w(dve, "rest1", n)
                alone(dve)
                dve.max(found[:, 8:16], adj_r1[:, :]).then_inc(s["top2"], 1)
                w(dve, "top2", n)
                alone(dve)
                dve.match_replace(adj_r2[:, :], found[:, 8:16], adj_r1[:, :], 0.0).then_inc(s["rest2"], 1)
                dve.max_index(found_idx[:, 8:16], found[:, 8:16], adj_r1[:, :])
                w(dve, "rest2", n)
                alone(dve)
                dve.max(found[:, 16:24], adj_r2[:, :]).then_inc(s["top3"], 1)
                w(dve, "top3", n)
                alone(dve)
                dve.tensor_scalar(over_bits[:, :], found[:, DIRECT:RANKS], 0.0, None, ALU.is_gt, ALU.add,
                                  accum_out=over_cnt[:, :]).then_inc(s["cnt"], 1)
                dve.max_index(found_idx[:, 16:24], found[:, 16:24], adj_r2[:, :]).then_inc(s["idx3"], 1)
                w(dve, "idx3", n)
                alone(dve)
                dve.tensor_copy(found[:, RANKS:2 * RANKS], found_idx[:, :]).then_inc(s["idxf"], 1)

            def place_overflow(g):
                n = g.at(3) + 1
                w(dve, "start_ready", n)
                w(dve, "idxf", n)
                start = found[:, 2 * RANKS:2 * RANKS + 1]
                dve.tensor_copy(start, p_start).then_inc(s["start_copied"], 1)
                w(dve, "start_copied", n)
                after(dve, "slot_ready", g, 2, 0)
                dve.tensor_scalar(slot_from[:, :], iota_row[:, :], start, None, ALU.is_ge)
                dve.tensor_tensor(over_end[:, bass.ds(g.at(3), 1)], start, over_cnt[:, :], ALU.add)\
                    .then_inc(s["from_ready"], 1)
                w(dve, "from_ready", n)
                dve.scalar_tensor_tensor(slot_of[:, :], iota_row[:, :], over_end[:, bass.ds(g.at(3), 1)],
                                         slot_from[:, :], ALU.is_lt, ALU.mult).then_inc(s["slot_ready"], 1)

            def finish_edges(g):
                q, n = g.mod(2, 2), g.at(2) + 1
                w(dve, "over_gathered", n)
                if not g.static or g.at(2) >= 2:
                    dve.wait_ge(edges_stored, 32 * (g.at(2) - 1))
                dve.tensor_scalar(rank_hit[:, :], iota_row[:, 0:OVER], p_over[:, 2 * RANKS:2 * RANKS + 1],
                                  iota_col[:, :], ALU.add, ALU.is_equal).then_inc(s["hits_ready"], 1)
                dve.tensor_copy(over_row[:, bass.ds(g.at(2), 1)], p_over[:, 2 * RANKS + 1:2 * RANKS + 2])
                dve.tensor_copy(last_rank[:, bass.ds(g.at(2), 1)], found[:, RANKS - 1:RANKS])
                dve.tensor_copy(ev[:, q, 0:DIRECT], found[:, 0:DIRECT])
                dve.tensor_copy(ei16[:, q, 0:DIRECT], found[:, RANKS:RANKS + DIRECT])
                w(dve, "hits_ready", n)
                dve.scalar_tensor_tensor(over_pick[:, 0, :], p_over[:, DIRECT:RANKS], 1.0, rank_hit[:, :],
                                         ALU.mult, ALU.mult, accum_out=ev[:, q, DIRECT:DIRECT + 1])
                dve.scalar_tensor_tensor(over_pick[:, 1, :], p_over[:, RANKS + DIRECT:2 * RANKS], 1.0,
                                         rank_hit[:, :], ALU.mult, ALU.mult,
                                         accum_out=ei[:, q, DIRECT:DIRECT + 1]).then_inc(s["picks_ready"], 1)
                w(dve, "picks_ready", n)
                dve.tensor_copy(ei16[:, q, DIRECT:DIRECT + 1], ei[:, q, DIRECT:DIRECT + 1]).then_inc(s["edges16"], 1)

            def body(pair):
                for i in range(per_pair):
                    u, g = unit(pair, i), graph(pair, i)
                    k_in = i % per_graph
                    if u.has(1):
                        q4 = u.mod(UNIT_BUFS, 1)
                        dve.wait_ge(unit_in[q4], unit_count(u, 1, q4))
                        after(dve, "rg_ready", u, -1, u0)
                        dve.tensor_scalar(pick[:, u.mod(2, 1), :], idx_bc[:, q4, :], iota_col[:, :], None,
                                          ALU.is_equal).then_inc(s["pick_ready"], 1)
                    if not dense and k_in == 0 and g.has(2):
                        finish_edges(g)
                    if not dense and k_in == 0 and g.has(0):
                        after_graph(dve, g, -2)
                        dve.tensor_scalar(over_t[:, g.mod(2), :], iota_row[:, :], over_row[:, bass.ds(g.at(), 1)], None,
                                          ALU.is_equal).then_inc(s["over_t_ready"], 1)
                    if u.has(1):
                        w(dve, "z_ready", u.at(1) + u0 + 1)
                        after(dve, "exp_ready", u, 0, u0)
                        c = clamped[:, :].rearrange("p (a n) -> p a n", a=2)
                        dve.tensor_scalar(c, zb[:, :, 0:HALF], b1c[:, :], CLAMP, ALU.add, ALU.min)\
                            .then_inc(s["clamped_ready"], 1)
                    if k_in == 1 and g.has(-1):
                        w(dve, "u_ready", g.at(-1) + g0 + 1)
                        after(dve, "uh_ready", g, -2, g0)
                        dve.tensor_scalar(t_u[:, :], p_u, bd1c[:, :], None, ALU.add).then_inc(s["u_read"], 1)
                    if k_in == 1 and g.has(-2):
                        w(dve, "out_ready", g.at(-2) + g0 + 1)
                        w(dve, "xb_ready", g.at(-2) + g0 + 1)
                        dve.tensor_tensor(xres[:, g.at(-2), :], p_out, xb[:, g.mod(2), :], ALU.add)\
                            .then_inc(s["res_ready"], 1)
                    if u.has(0):
                        q, q4 = u.mod(2), u.mod(UNIT_BUFS)
                        w(dve, "wf_ready", u.at() + u0 + 1)
                        w(dve, "rfe_ready", u.at() + u0 + 1)
                        w(dve, "valsq_ready", u.at() + u0 + 1)
                        after(dve, "summed", u, -2, u0)
                        for r in range(R):
                            last = dve.scalar_tensor_tensor(
                                msg[:, q, r * P:(r + 1) * P], column(wf, r), val_sq[:, q4, r:r + 1],
                                rfe[:, q, r * P:(r + 1) * P], ALU.mult, ALU.mult)
                        last.then_inc(s["msg_ready"], 1)
                    if k_in == 1 and g.has(-1):
                        w(dve, "u_read", g.at(-1) + g0 + 1)
                        after(dve, "uexp_ready", g, -2, g0)
                        dve.tensor_scalar(t_cl[:, :], t_u[:, :], CLAMP, None, ALU.min)\
                            .then_inc(s["uclamped_ready"], 1)
                    if k_in == 0 and g.has(1):
                        w(dve, "rfhi_ready", g.at(1) + g0 + 1)
                        after_graph(dve, g, -1)
                        after(dve, "rflo_ready", g, 0, g0)
                        dve.tensor_tensor(rf_r1[:, :], p_rf, rf_hi[:, g.mod(2, 1), :], ALU.subtract)\
                            .then_inc(s["rfr1_ready"], 1)
                        dve.tensor_tensor(rfb[:, g.mod(2, 1), :], p_rf, b2bc[:, :], ALU.mult)\
                            .then_inc(s["rfb_ready"], 1)
                        w(dve, "rfr1_ready", g.at(1) + g0 + 1)
                        dve.tensor_copy(rf_mid[:, g.mod(2, 1), :], rf_r1[:, :]).then_inc(s["rfmid_ready"], 1)
                        w(dve, "rfmid_ready", g.at(1) + g0 + 1)
                        dve.tensor_tensor(rf_lo[:, g.mod(2, 1), :], rf_r1[:, :], rf_mid[:, g.mod(2, 1), :],
                                          ALU.subtract).then_inc(s["rflo_ready"], 1)
                    if not dense and k_in == 0 and g.has(3):
                        rank_edges(g)
                    if not dense and k_in == 1 and g.has(3):
                        place_overflow(g)
                    if k_in == 0 and g.has(-2):
                        w(dve, "ulog_ready", g.at(-2) + g0 + 1)
                        after(dve, "out_ready", g, -3, g0)
                        dve.tensor_tensor(t_h[:, :], t_u[:, :], t_lg[:, :], ALU.max).then_inc(s["uh_ready"], 1)
                    if u.has(1):
                        w(dve, "log_ready", u.at(1) + u0 + 1)
                        after(dve, "wf_ready", u, -1, u0)
                        h = hid[:, u.mod(2, 1), :].rearrange("p (a n) -> p a n", a=2)
                        l = logd[:, :].rearrange("p (a n) -> p a n", a=2)
                        dve.scalar_tensor_tensor(h, zb[:, :, 0:HALF], b1c[:, :], l, ALU.add, ALU.max)\
                            .then_inc(s["hid_ready"], 1)
            schedule(dve, body)

    with ExitStack() as c1:
        run(c1.enter_context(nc.Block()), dense=False)

    with ExitStack() as c1:
        viol = s["top1"]
        chk = [phase_semaphore(nc, c0, k, f"chk{i}") for i in range(6)]
        bad = c1.enter_context(nc.sbuf_tensor("bad", [P, 3, B], F32))
        badn = c1.enter_context(nc.sbuf_tensor("badn", [P, 1], F32))
        onec = c1.enter_context(nc.sbuf_tensor("onec", [P, 1], F32))
        block = c1.enter_context(nc.Block())

        @block.vector
        def _(dve):
            dve.memset(onec[:, :], 1.0)
            dve.tensor_scalar(bad[:, 0, :], over_end[:, :], float(P), None, ALU.is_gt)
            dve.tensor_scalar(bad[:, 1, :], last_rank[:, :], 0.0, None, ALU.is_gt)
            dve.tensor_scalar(bad[:, 2, :], least[:, :], 0.0, None, ALU.is_lt).then_inc(chk[0], 1)
            dve.wait_ge(chk[0], 1)
            dve.tensor_reduce(badn[:, :], bad[:, :, :], AX.XY, ALU.add).then_inc(chk[1], 1)
            dve.wait_ge(chk[2], 1)
            dve.tensor_copy(flag[:, :], p_flag)

        @block.tensor
        def _(pe):
            pe.wait_ge(chk[1], 1)
            pe.matmul(p_flag, onec[:, :], badn[:, :], start=True, stop=True).then_inc(chk[2], 1)

    if k.get("no_dense"):
        return

    class Guarded:

        def __init__(self, block):
            self.block = block

        def _under_flag(self, of):
            def wrap(program):
                def guarded(eng):
                    overflow = eng.value_load(flag[0:1, 0:1], min_val=0, max_val=3 * B * P)
                    with eng.If(overflow > 0):
                        program(eng)
                of(guarded)
            return wrap

        sync = property(lambda self: self._under_flag(self.block.sync))
        gpsimd = property(lambda self: self._under_flag(self.block.gpsimd))
        scalar = property(lambda self: self._under_flag(self.block.scalar))
        tensor = property(lambda self: self._under_flag(self.block.tensor))
        vector = property(lambda self: self._under_flag(self.block.vector))

    with ExitStack() as c1:
        run(Guarded(c1.enter_context(nc.Block())), dense=True)


def layers12(nc, a, k):
    ctx = k["ctx"]
    xres, ident, deg, held = k["xres"], k["ident"], k["deg"], k["held"]
    dyn, agg = k["dyn"], k["agg"]
    NEG = -3.0e38

    with ExitStack() as c0:
        def sb(name, shape, dt=F32):
            return c0.enter_context(nc.sbuf_tensor("m_" + name, shape, dt))

        def ps(name):
            return c0.enter_context(nc.psum_tensor("m_" + name, [P, G, P], F32))

        wq_t, wk_t, wv = sb("wq_t", [P, P]), sb("wk_t", [P, P]), sb("wv", [P, P])
        w_layer, w_layer_t = sb("w_layer", [P, P]), sb("w_layer_t", [P, P])
        w_self, w_neigh = sb("w_self", [P, 1]), sb("w_neigh", [P, 1])
        conv_w = sb("conv_w", [P, 3, P])
        rows = sb("rows", [1, 4, P])
        mask = sb("mask", [P, B])
        wqk = sb("wqk", [P, P])
        att_self = sb("att_self", [P, 1])
        att_neigh = sb("att_neigh", [P, P])
        ones = sb("ones", [P, P])
        gamma4, beta4, bl4 = sb("gamma4", [P, G, P]), sb("beta4", [P, G, P]), sb("bl4", [P, G, P])
        conv_b4 = sb("conv_b4", [P, G, P])
        minus_half, dsafe, dpos, dpow = (sb(n, [P, G]) for n in ("minus_half", "dsafe", "dpos", "dpow"))

        adj_g, adjt_g = sb("adj_g", [P, 2, G, P]), sb("adjt_g", [P, 2, G, P])
        stats = {n: sb("stats_" + n, [P, G, 6]) for n in ("n0", "no", "n1", "n2")}
        mv = {n: sb("mv_" + n, [P, G, 2]) for n in stats}
        veps = {n: sb("veps_" + n, [P, G]) for n in stats}
        rstd = {n: sb("rstd_" + n, [P, G]) for n in stats}
        scratch = iter(range(B // G))

        def work():
            i = next(scratch)
            return k["xin"][:, i * G:(i + 1) * G, :]

        x1, x1b, x1t, qt, val = (sb(n, [P, G, P]) for n in ("x1", "x1b", "x1t", "qt", "val"))
        score = sb("score", [P, G, P])
        rest, esc, prob, prob_t = (work() for _ in range(4))
        top = sb("top", [P, G, 8])
        negmax, psum, rsum = sb("negmax", [P, G]), sb("psum", [P, G]), sb("rsum", [P, G])
        o1, o1n, o1g, r1 = (work() for _ in range(4))
        x2 = sb("x2", [P, 2, G, P])
        nb = sb("nb", [P, 2, G, P])
        x2t, hl, e2t = (sb(n, [P, G, P]) for n in ("x2t", "hl", "e2t"))
        lsum, leaky, logit, e2 = (work() for _ in range(4))
        a_self = sb("a_self", [P, G])
        negmax2, psum2, rsum2, rmask = (sb(n, [P, G]) for n in ("negmax2", "psum2", "rsum2", "rmask"))
        bm, xb2, o2, r2 = (work() for _ in range(4))
        xpad, xs, adj_i = sb("xpad", [P, G, P + 2]), sb("xs", [P, G, P]), sb("adj_i", [P, G, P])
        dinv = k["dinv"]

        pa, pb, pc = ps("pa"), ps("pb"), ps("pc")
        pd, pe_h, pf = ps("pd"), ps("pe_h"), ps("pf")
        pg, ph = ps("pg"), ps("ph")

        names = (
            "n0_mv n0_veps n0_rstd x1 x1b x1t_p x1t qt_p qt val_p val s_p score top negmax rest esc prob rsum "
            "probt_p probt o1_p o1 no_mv no_veps no_rstd o1n o1g r1 n1_mv n1_veps n1_rstd x2 "
            "nb deg x2t_p x2t as_p a_self h_p hl an_p lsum leaky logit negmax2 e2 rsum2 rmask e2t_p e2t o2_p o2 "
            "bm xb2 r2 n2_mv n2_veps n2_rstd x3 "
            "dsafe dpos dpow dinv xpad xs adj_i conv_p dyn agg_p agg n0_st no_st n1_st n2_st"
        ).split()
        s = {n: phase_semaphore(nc, c0, k, "m_" + n) for n in names}
        w_in = phase_semaphore(nc, c0, k, "m_w_in")
        adj_in = [phase_semaphore(nc, c0, k, f"m_adj_in{i}") for i in range(2)]
        adjt_in = [phase_semaphore(nc, c0, k, f"m_adjt_in{i}") for i in range(2)]
        pre = [phase_semaphore(nc, c0, k, f"m_pre{i}") for i in range(4)]

        with ExitStack() as c1:
            block = c1.enter_context(nc.Block())

            @block.sync
            def _(sp):
                for dst, src in ((wq_t, "wqt"), (wk_t, "wkt"), (wv, "wv"), (w_layer, "w_layer"),
                                 (w_layer_t, "w_layer_t"), (w_self, "w_self"), (w_neigh, "w_neigh"),
                                 (mask, "mask_rows")):
                    sp.dma_start(dst[:, :], a[src]).then_inc(w_in, 16)
                sp.dma_start(conv_w[:, :, :], a["conv_wt"]).then_inc(w_in, 16)
                for j, src in enumerate(("gamma_row", "beta_row", "b_layer_row", "conv_b_row")):
                    sp.dma_start(rows[:, j, :], a[src]).then_inc(w_in, 16)

            @block.vector
            def _(dve):
                dve.memset(minus_half[:, :], -0.5)
                dve.memset(xpad[:, :, :], 0.0)
                dve.memset(ones[:, :], 1.0).then_inc(pre[0], 1)
                dve.wait_ge(pre[1], 1)
                dve.tensor_scalar(wqk[:, :], pa[:, 0, :], float(P) ** -0.5, None, ALU.mult)
                dve.tensor_copy(att_self[:, :], pa[:, 1, 0:1])
                dve.wait_ge(pre[0], 1)
                dve.tensor_scalar(att_neigh[:, :], ones[:, :], pa[:, 2, 0:1], None, ALU.mult)
                for j, dst in enumerate((gamma4, beta4, bl4, conv_b4)):
                    dve.tensor_copy(dst[:, :, :], pb[:, j:j + 1, :].broadcast_to((P, G, P)))

            @block.tensor
            def _(pe):
                pe.wait_ge(w_in, 16 * 13)
                pe.wait_ge(pre[0], 1)
                pe.matmul(pa[:, 0, :], wq_t[:, :], wk_t[:, :], start=True, stop=True)
                pe.matmul(pa[:, 1, 0:1], w_layer_t[:, :], w_self[:, :], start=True, stop=True)
                pe.matmul(pa[:, 2, 0:1], w_layer_t[:, :], w_neigh[:, :], start=True, stop=True)
                for j in range(4):
                    last = pe.matmul(pb[:, j, :], ones[0:1, :], rows[:, j, :], start=True, stop=True)
                last.then_inc(pre[1], 1)

        NGR = B // G

        def schedule(eng, body):
            pairs(eng, (0,), (1, NGR // 2 - 1), (NGR // 2 - 1, NGR // 2), body)

        def steps(pair):
            for i in range(2):
                g = Steps(pair, i, 2, NGR)
                yield g, g.has(0), g.has(-1), g.has(-2)

        def w(eng, name, g, d=0):
            eng.wait_ge(s[name], g.at(d) + 1)

        def after(eng, name, g, d):
            if not g.static or g.at(d) >= 0:
                eng.wait_ge(s[name], min(g.at(d), NGR - 1) + 1 if g.static else g.at(d) + 1)

        def landed(eng, sems, g, d=0):
            eng.wait_ge(sems[g.mod(2, d)], g.pair * 16 + 16 * ((g.inner + d) // 2 + 1))

        with ExitStack() as c1:
            block = c1.enter_context(nc.Block())

            def four(g, d=0):
                return bass.ds(g.at(d) * G, G)

            @block.sync
            def _(sp):
                def load(g, d):
                    q = g.mod(2, d)
                    sp.dma_start(adj_g[:, q, :, :], a["adj_rows"][:, four(g, d), :]).then_inc(adj_in[q], 16)

                def load_t(g, d):
                    q = g.mod(2, d)
                    sp.dma_start(adjt_g[:, q, :, :], a["adj_t"][:, four(g, d), :]).then_inc(adjt_in[q], 16)

                def body(pair):
                    for g, one, two, three in steps(pair):
                        if g.static and g.at() == 0:
                            load(g, 0)
                        if g.has(1):
                            after(sp, "score", g, -1)
                            after(sp, "deg", g, -1)
                            after(sp, "nb", g, -1)
                            sp.sem_inc(held["SP"], 1)
                            load(g, 1)
                        if g.has(-1):
                            after(sp, "adj_i", g, -3)
                            sp.sem_inc(held["SP"], 1)
                            load_t(g, -1)
                schedule(sp, body)

            @block.gpsimd
            def _(pool):
                def rstd_of(g, d, n):
                    w(pool, n + "_mv", g, d)
                    pool.sem_inc(held["Pool"], 1)
                    pool.tensor_scalar(veps[n][:, :], mv[n][:, :, 1], EPS, None, ALU.add).then_inc(s[n + "_veps"], 1)
                    w(pool, n + "_veps", g, d)
                    pool.tensor_tensor(rstd[n][:, :], veps[n][:, :], minus_half[:, :], ALU.pow)\
                        .then_inc(s[n + "_rstd"], 1)

                def body(pair):
                    for g, one, two, three in steps(pair):
                        if one:
                            rstd_of(g, 0, "n0")
                        if three:
                            w(pool, "x3", g, -2)
                            after(pool, "conv_p", g, -3)
                            pool.sem_inc(held["Pool"], 1)
                            pool.tensor_copy(xpad[:, :, 1:P + 1], xres[:, four(g, -2), :]).then_inc(s["xpad"], 1)
                            landed(pool, adjt_in, g, -2)
                            after(pool, "agg_p", g, -3)
                            pool.tensor_tensor(adj_i[:, :, :], adjt_g[:, g.mod(2, -2), :, :],
                                               ident[:, :].unsqueeze(1).broadcast_to((P, G, P)), ALU.add)\
                                .then_inc(s["adj_i"], 1)
                        if one:
                            landed(pool, adj_in, g)
                            after(pool, "logit", g, -2)
                            pool.sem_inc(held["Pool"], 1)
                            pool.tensor_scalar(nb[:, g.mod(2), :, :], adj_g[:, g.mod(2), :, :], -1.0, 1.0e10,
                                               ALU.add, ALU.mult).then_inc(s["nb"], 1)
                            w(pool, "deg", g)
                            after(pool, "dpow", g, -1)
                            pool.sem_inc(held["Pool"], 1)
                            pool.tensor_scalar(dsafe[:, :], deg[:, g.mod(2), :], 1.0, 1.2e-38, ALU.add, ALU.max)\
                                .then_inc(s["dsafe"], 1)
                            after(pool, "dinv", g, -1)
                            pool.sem_inc(held["Pool"], 1)
                            pool.tensor_scalar(dpos[:, :], deg[:, g.mod(2), :], 1.0, 0.0, ALU.add, ALU.is_gt)\
                                .then_inc(s["dpos"], 1)
                            w(pool, "dsafe", g)
                            pool.tensor_tensor(dpow[:, :], dsafe[:, :], minus_half[:, :], ALU.pow)\
                                .then_inc(s["dpow"], 1)
                            w(pool, "dpow", g)
                            w(pool, "dpos", g)
                            pool.sem_inc(held["Pool"], 1)
                            pool.tensor_tensor(dinv[:, four(g)], dpow[:, :], dpos[:, :], ALU.mult)\
                                .then_inc(s["dinv"], 1)
                            w(pool, "x1", g)
                            after(pool, "r1", g, -1)
                            pool.tensor_tensor(x1b[:, :, :], x1[:, :, :], beta4[:, :, :], ALU.add)\
                                .then_inc(s["x1b"], 1)
                        if two:
                            after(pool, "xb2", g, -2)
                            pool.sem_inc(held["Pool"], 1)
                            pool.tensor_tensor(bm[:, :, :], bl4[:, :, :],
                                               mask[:, four(g, -1)].unsqueeze(2).broadcast_to((P, G, P)), ALU.mult)\
                                .then_inc(s["bm"], 1)
                            w(pool, "bm", g, -1)
                            w(pool, "x2", g, -1)
                            after(pool, "r2", g, -2)
                            pool.tensor_tensor(xb2[:, :, :], bm[:, :, :], x2[:, g.mod(2, -1), :, :], ALU.add)\
                                .then_inc(s["xb2"], 1)
                            rstd_of(g, -1, "n2")
                        if one:
                            rstd_of(g, 0, "no")
                            w(pool, "o1n", g)
                            after(pool, "r1", g, -1)
                            pool.tensor_tensor(o1g[:, :, :], o1n[:, :, :], gamma4[:, :, :], ALU.mult)\
                                .then_inc(s["o1g"], 1)
                            w(pool, "o1g", g)
                            w(pool, "x1b", g)
                            after(pool, "x2", g, -1)
                            pool.tensor_tensor(r1[:, :, :], o1g[:, :, :], x1b[:, :, :], ALU.add).then_inc(s["r1"], 1)
                            rstd_of(g, 0, "n1")
                schedule(pool, body)

            @block.scalar
            def _(act):
                act.preload_act_table_set("natural_log_exp_and_others")

                def evac(g, d, dst, src, ready, done):
                    w(act, ready, g, d)
                    return act.activation(dst, src, ACT.Copy).then_inc(s[done], 1)

                def body(pair):
                    for g, one, two, three in steps(pair):
                        if two:
                            after(act, "an_p", g, -2)
                            evac(g, -1, x2t[:, :, :], pd[:, :, :], "x2t_p", "x2t")
                            after(act, "o2_p", g, -2)
                            evac(g, -1, hl[:, :, :], pe_h[:, :, :], "h_p", "hl")
                        if one:
                            after(act, "s_p", g, -1)
                            evac(g, 0, x1t[:, :, :], pa[:, :, :], "x1t_p", "x1t")
                            evac(g, 0, qt[:, :, :], pb[:, :, :], "qt_p", "qt")
                            after(act, "o1_p", g, -1)
                            evac(g, 0, val[:, :, :], pc[:, :, :], "val_p", "val")
                        if two:
                            w(act, "negmax2", g, -1)
                            after(act, "e2t_p", g, -2)
                            after(act, "rsum2", g, -2)
                            for j in range(G):
                                last = act.activation(e2[:, j, :], logit[:, j, :], ACT.Exp, bias=negmax2[:, j:j + 1],
                                                      accum_out=psum2[:, j:j + 1])
                            last.then_inc(s["e2"], 1)
                        if one:
                            w(act, "negmax", g)
                            after(act, "prob", g, -1)
                            for j in range(G):
                                last = act.activation(esc[:, j, :], score[:, j, :], ACT.Exp, bias=negmax[:, j:j + 1])
                            last.then_inc(s["esc"], 1)
                        if two:
                            evac(g, -1, e2t[:, :, :], pd[:, :, :], "e2t_p", "e2t")
                        if three:
                            evac(g, -2, agg[:, four(g, -2), :], ph[:, :, :], "agg_p", "agg")
                        if one:
                            evac(g, 0, prob_t[:, :, :], pb[:, :, :], "probt_p", "probt")
                schedule(act, body)

            @block.tensor
            def _(pe):
                def body(pair):
                    for g, one, two, three in steps(pair):
                        if two:
                            w(pe, "x2", g, -1)
                            after(pe, "e2t", g, -2)
                            for j in range(G):
                                last = pe.transpose(pd[:, j, :], x2[:, g.mod(2, -1), j, :], ident[:, :])
                            last.then_inc(s["x2t_p"], 1)
                            w(pe, "x2t", g, -1)
                            for j in range(G):
                                last = pe.matmul(pd[:, 0, j:j + 1], x2t[:, j, :], att_self[:, :], start=True, stop=True)
                            last.then_inc(s["as_p"], 1)
                            for j in range(G):
                                last = pe.matmul(pe_h[:, j, :], x2t[:, j, :], w_layer[:, :], start=True, stop=True)
                            last.then_inc(s["h_p"], 1)
                            after(pe, "o2", g, -2)
                            pe.matmul(pf[:, :, :], att_neigh[:, :], x2t[:, :, :], start=True, stop=True)\
                                .then_inc(s["an_p"], 1)
                        if one:
                            w(pe, "x1", g)
                            after(pe, "o1", g, -1)
                            for j in range(G):
                                last = pe.transpose(pa[:, j, :], x1[:, j, :], ident[:, :])
                            last.then_inc(s["x1t_p"], 1)
                            w(pe, "x1t", g)
                            pe.matmul(pb[:, :, :], wqk[:, :], x1t[:, :, :], start=True, stop=True)\
                                .then_inc(s["qt_p"], 1)
                            after(pe, "val", g, -1)
                            for j in range(G):
                                last = pe.matmul(pc[:, j, :], x1t[:, j, :], wv[:, :], start=True, stop=True)
                            last.then_inc(s["val_p"], 1)
                            w(pe, "qt", g)
                            for j in range(G):
                                last = pe.matmul(pa[:, j, :], qt[:, j, :], x1t[:, j, :], start=True, stop=True)
                            last.then_inc(s["s_p"], 1)
                        if three:
                            w(pe, "xpad", g, -2)
                            after(pe, "dyn", g, -3)
                            for j in range(G):
                                for kk in range(3):
                                    last = pe.matmul(pg[:, j, :], xpad[:, j, kk:kk + P], conv_w[:, kk, :],
                                                     start=kk == 0, stop=kk == 2)
                            last.then_inc(s["conv_p"], 1)
                            w(pe, "xs", g, -2)
                            w(pe, "adj_i", g, -2)
                            after(pe, "agg", g, -3)
                            for j in range(G):
                                last = pe.matmul(ph[:, j, :], xs[:, j, :], adj_i[:, j, :], start=True, stop=True)
                            last.then_inc(s["agg_p"], 1)
                        if two:
                            w(pe, "e2", g, -1)
                            w(pe, "a_self", g, -1)
                            for j in range(G):
                                last = pe.transpose(pd[:, j, :], e2[:, j, :], ident[:, :])
                            last.then_inc(s["e2t_p"], 1)
                            w(pe, "e2t", g, -1)
                            w(pe, "hl", g, -1)
                            w(pe, "lsum", g, -1)
                            for j in range(G):
                                last = pe.matmul(pf[:, j, :], e2t[:, j, :], hl[:, j, :], start=True, stop=True)
                            last.then_inc(s["o2_p"], 1)
                        if one:
                            w(pe, "prob", g)
                            for j in range(G):
                                last = pe.transpose(pb[:, j, :], prob[:, j, :], ident[:, :])
                            last.then_inc(s["probt_p"], 1)
                            w(pe, "probt", g)
                            w(pe, "val", g)
                            w(pe, "score", g)
                            for j in range(G):
                                last = pe.matmul(pa[:, j, :], prob_t[:, j, :], val[:, j, :], start=True, stop=True)
                            last.then_inc(s["o1_p"], 1)
                schedule(pe, body)

            @block.vector
            def _(dve):
                def moments(g, d, n, x):
                    after(dve, n + "_mv", g, d - 1)
                    for j in range(G):
                        last = dve.bn_stats(stats[n][:, j, :], x(j))
                    last.then_inc(s[n + "_st"], 1)
                    w(dve, n + "_st", g, d)
                    after(dve, n + "_rstd", g, d - 1)
                    after(dve, {"n0": "x1", "no": "o1n", "n1": "x2", "n2": "x3"}[n], g, d - 1)
                    dve.sem_inc(held["DVE"], 1)
                    for j in range(G):
                        last = dve.bn_aggr(mv[n][:, j, :], stats[n][:, j, :])
                    last.then_inc(s[n + "_mv"], 1)

                def normalise(g, d, n, dst, x, done):
                    w(dve, n + "_rstd", g, d)
                    for j in range(G):
                        last = dve.tensor_scalar(dst(j), x(j), mv[n][:, j, 0:1], rstd[n][:, j:j + 1],
                                                 ALU.subtract, ALU.mult)
                    last.then_inc(s[done], 1)

                def bc(t):
                    return t.unsqueeze(2).broadcast_to((P, G, P))

                def one_graph(g, d, j):
                    return bass.ds(g.at(d) * G + j, 1)

                def body(pair):
                    for g, one, two, three in steps(pair):
                        if three:
                            after(dve, "agg_p", g, -3)
                            w(dve, "x3", g, -2)
                            w(dve, "dinv", g, -2)
                            dve.tensor_tensor(xs[:, :, :], xres[:, four(g, -2), :], bc(dinv[:, four(g, -2)]), ALU.mult)\
                                .then_inc(s["xs"], 1)
                        if one:
                            x0 = lambda j: xres[:, one_graph(g, 0, j), :].rearrange("p a n -> p (a n)")
                            moments(g, 0, "n0", x0)
                        if two:
                            w(dve, "as_p", g, -1)
                            after(dve, "lsum", g, -2)
                            dve.tensor_copy(a_self[:, :], pd[:, 0, 0:G]).then_inc(s["a_self"], 1)
                        if one:
                            after(dve, "x1t_p", g, -1)
                            after(dve, "x1b", g, -1)
                            normalise(g, 0, "n0", lambda j: x1[:, j, :], x0, "x1")
                        if two:
                            w(dve, "an_p", g, -1)
                            w(dve, "a_self", g, -1)
                            after(dve, "leaky", g, -2)
                            dve.tensor_tensor(lsum[:, :, :], pf[:, :, :], bc(a_self[:, :]), ALU.add)\
                                .then_inc(s["lsum"], 1)
                            w(dve, "lsum", g, -1)
                            after(dve, "logit", g, -2)
                            dve.scalar_tensor_tensor(leaky[:, :, :], lsum[:, :, :], 0.2, lsum[:, :, :], ALU.mult,
                                                     ALU.max).then_inc(s["leaky"], 1)
                            w(dve, "leaky", g, -1)
                            w(dve, "nb", g, -1)
                            after(dve, "e2", g, -2)
                            dve.tensor_tensor(logit[:, :, :], leaky[:, :, :], nb[:, g.mod(2, -1), :, :], ALU.add)\
                                .then_inc(s["logit"], 1)
                            w(dve, "logit", g, -1)
                            dve.tensor_reduce(negmax2[:, :], logit[:, :, :], AX.X, ALU.max, negate=True)\
                                .then_inc(s["negmax2"], 1)
                        if one:
                            landed(dve, adj_in, g)
                            after(dve, "dinv", g, -2)
                            dve.tensor_reduce(deg[:, g.mod(2), :], adj_g[:, g.mod(2), :, :], AX.X, ALU.add)\
                                .then_inc(s["deg"], 1)
                            w(dve, "s_p", g)
                            after(dve, "esc", g, -1)
                            after(dve, "rest", g, -1)
                            dve.tensor_tensor(score[:, :, :], pa[:, :, :], adj_g[:, g.mod(2), :, :], ALU.add)\
                                .then_inc(s["score"], 1)
                            after(dve, "rest", g, -1)
                            w(dve, "score", g)
                            dve.sem_inc(held["DVE"], 1)
                            for j in range(G):
                                last = dve.max(top[:, j, :], score[:, j, :])
                            last.then_inc(s["top"], 1)
                            w(dve, "top", g)
                            dve.tensor_scalar(negmax[:, :], top[:, :, 0], -1.0, None, ALU.mult)\
                                .then_inc(s["negmax"], 1)
                            after(dve, "prob", g, -1)
                            dve.sem_inc(held["DVE"], 1)
                            for j in range(G):
                                last = dve.match_replace(rest[:, j, :], top[:, j, :], score[:, j, :], NEG)
                            last.then_inc(s["rest"], 1)
                        if three:
                            w(dve, "conv_p", g, -2)
                            dve.tensor_tensor(dyn[:, :, four(g, -2)].rearrange("p t b -> p b t"), pg[:, :, :],
                                              conv_b4[:, :, :], ALU.add).then_inc(s["dyn"], 1)
                        if two:
                            w(dve, "e2", g, -1)
                            dve.reciprocal(rsum2[:, :], psum2[:, :]).then_inc(s["rsum2"], 1)
                            w(dve, "rsum2", g, -1)
                            after(dve, "o2", g, -2)
                            dve.tensor_tensor(rmask[:, :], rsum2[:, :], mask[:, four(g, -1)], ALU.mult)\
                                .then_inc(s["rmask"], 1)
                        if one:
                            w(dve, "esc", g)
                            w(dve, "rest", g)
                            after(dve, "probt_p", g, -1)
                            after(dve, "rsum", g, -1)
                            for j in range(G):
                                last = dve.scalar_tensor_tensor(prob[:, j, :], rest[:, j, :], -1.0e38, esc[:, j, :],
                                                                ALU.is_lt, ALU.mult, accum_out=psum[:, j:j + 1])
                            last.then_inc(s["prob"], 1)
                            w(dve, "prob", g)
                            after(dve, "o1", g, -1)
                            dve.reciprocal(rsum[:, :], psum[:, :]).then_inc(s["rsum"], 1)
                        if two:
                            w(dve, "o2_p", g, -1)
                            w(dve, "rmask", g, -1)
                            after(dve, "r2", g, -2)
                            dve.tensor_tensor(o2[:, :, :], pf[:, :, :], bc(rmask[:, :]), ALU.mult).then_inc(s["o2"], 1)
                            w(dve, "o2", g, -1)
                            w(dve, "xb2", g, -1)
                            after(dve, "x3", g, -2)
                            dve.tensor_tensor(r2[:, :, :], o2[:, :, :], xb2[:, :, :], ALU.add).then_inc(s["r2"], 1)
                            w(dve, "r2", g, -1)
                            moments(g, -1, "n2", lambda j: r2[:, j, :])
                        if one:
                            w(dve, "o1_p", g)
                            w(dve, "rsum", g)
                            after(dve, "o1n", g, -1)
                            dve.tensor_tensor(o1[:, :, :], pa[:, :, :], bc(rsum[:, :]), ALU.mult).then_inc(s["o1"], 1)
                            w(dve, "o1", g)
                            moments(g, 0, "no", lambda j: o1[:, j, :])
                        if two:
                            normalise(g, -1, "n2", lambda j: xres[:, one_graph(g, -1, j), :]
                                      .rearrange("p a n -> p (a n)"), lambda j: r2[:, j, :], "x3")
                        if one:
                            after(dve, "o1g", g, -1)
                            normalise(g, 0, "no", lambda j: o1n[:, j, :], lambda j: o1[:, j, :], "o1n")
                        if one:
                            w(dve, "r1", g)
                            moments(g, 0, "n1", lambda j: r1[:, j, :])
                            after(dve, "x2t_p", g, -2)
                            after(dve, "xb2", g, -2)
                            normalise(g, 0, "n1", lambda j: x2[:, g.mod(2), j, :], lambda j: r1[:, j, :], "x2")
                schedule(dve, body)

        clear_semaphores(nc, k)


def lstm(nc, a, k):
    dyn, agg, xres, ident, dinv, out, held = (k[n] for n in ("dyn", "agg", "xres", "ident", "dinv", "out", "held"))
    hs = k["xin"][:, :, :].rearrange("p g n -> p (g n)").rearrange("p (t b) -> p t b", b=B)
    with ExitStack() as c0:
        def sb(name, shape, dt=F32):
            return c0.enter_context(nc.sbuf_tensor("r_" + name, shape, dt))

        def sem(name):
            return phase_semaphore(nc, c0, k, "r_" + name)

        w_ih, w_hh = sb("w_ih", [P, 4, P]), sb("w_hh", [P, 4, P])
        b_ih, b_hh = sb("b_ih", [1, 4, P]), sb("b_hh", [1, 4, P])
        bias = sb("bias", [1, 4, P])
        ones = sb("ones", [1, 2 * B])
        h0 = sb("h0", [P, B])
        gates = sb("gates", [P, 4, B])
        cell = sb("cell", [P, B])
        keep, new, tanh_c = sb("keep", [P, B]), sb("new", [P, B]), sb("tanh_c", [P, B])
        weights_in, prep_a, prep_b = sem("weights_in"), sem("prep_a"), sem("prep_b")
        x_part, z_ready, gates_ready, keep_ready, new_ready, cell_ready, tanh_ready, h_ready = (
            sem(n) for n in ("x_part", "z_ready", "gates_ready", "keep_ready", "new_ready", "cell_ready",
                             "tanh_ready", "h_ready"))
        zp = [c0.enter_context(nc.psum_tensor(f"r_z{i}", [P, 4, 2 * B], F32)) for i in range(2)]
        I_, F_, G_, O_ = range(4)

        with ExitStack() as c1:
            block = c1.enter_context(nc.Block())

            @block.sync
            def _(sp):
                for dst, src in ((w_ih, "w_iht"), (w_hh, "w_hht"), (b_ih, "b_ih_row"), (b_hh, "b_hh_row")):
                    sp.dma_start(dst[:, :, :].rearrange("p a n -> p (a n)"), a[src]).then_inc(weights_in, 16)

            @block.vector
            def _(dve):
                dve.memset(h0[:, :], 0.0)
                dve.memset(cell[:, :], 0.0)
                dve.memset(ones[:, :], 1.0)
                dve.wait_ge(weights_in, 64)
                dve.tensor_tensor(bias[:, :, :], b_ih[:, :, :], b_hh[:, :, :], ALU.add).then_inc(prep_a, 1)
                dve.wait_ge(prep_a, 1)
                for q in (I_, F_, O_):
                    dve.tensor_scalar(bias[:, q, :], bias[:, q, :], 0.5, None, ALU.mult)
                    dve.tensor_scalar(w_ih[:, q, :], w_ih[:, q, :], 0.5, None, ALU.mult)
                for q in range(4):
                    dve.tensor_scalar(w_hh[:, q, :], w_hh[:, q, :], 0.5 if q == G_ else 0.25, None, ALU.mult)

        with ExitStack() as c1:
            block = c1.enter_context(nc.Block())

            def quads(eng, body):
                body(0, True, False)
                with eng.Fori(1, P // 4 - 1) as quad:
                    body(quad * 4, False, False)
                body(P - 4, False, True)

            @block.tensor
            def _(pe):
                def inputs(t, bank):
                    z = zp[bank]
                    for q in range(4):
                        pe.matmul(z[:, q, :], bias[:, q, :], ones[:, :], start=q == 0, stop=False,
                                  skip_group_check=True)
                        pe.matmul(z[:, q, :], w_ih[:, q, :], dyn[:, bass.ds(t, 2), :], start=False, stop=False,
                                  skip_group_check=True)

                def recurrence(t, j, h):
                    z = zp[j // 2]
                    for q in (G_, I_, F_, O_):
                        last = pe.matmul(z[:, q, (j % 2) * B:(j % 2 + 1) * B], w_hh[:, q, :], h, start=False,
                                         stop=True, skip_group_check=True)
                    last.then_inc(z_ready, 1)

                def body(t, first, final):
                    if first:
                        inputs(0, 0)
                    for j in range(4):
                        if first and j == 0:
                            h = h0[:, :]
                        else:
                            pe.wait_ge(h_ready, t + j)
                            h = hs[:, bass.ds(t + (j - 1), 1), :]
                        recurrence(t, j, h)
                        if j == 0:
                            inputs(t + 2, 1)
                        if j == 2 and not final:
                            inputs(t + 4, 0)
                quads(pe, body)

            @block.scalar
            def _(act):
                def body(t, first, final):
                    for j in range(4):
                        act.wait_ge(z_ready, t + (j + 1))
                        if not (first and j == 0):
                            act.wait_ge(h_ready, t + j)
                        act.activation(gates[:, :, :], zp[j // 2][:, :, (j % 2) * B:(j % 2 + 1) * B], ACT.Tanh)\
                            .then_inc(gates_ready, 1)
                        act.wait_ge(cell_ready, t + (j + 1))
                        act.activation(tanh_c[:, :], cell[:, :], ACT.Tanh, scale=0.5).then_inc(tanh_ready, 1)
                quads(act, body)

            @block.vector
            def _(dve):
                def body(t, first, final):
                    for j in range(4):
                        n = t + (j + 1)
                        dve.wait_ge(gates_ready, n)
                        dve.scalar_tensor_tensor(keep[:, :], gates[:, F_, :], 1.0, cell[:, :], ALU.add, ALU.mult)
                        dve.scalar_tensor_tensor(new[:, :], gates[:, I_, :], 1.0, gates[:, G_, :], ALU.add, ALU.mult)\
                            .then_inc(new_ready, 1)
                        dve.wait_ge(new_ready, n)
                        dve.scalar_tensor_tensor(cell[:, :], keep[:, :], 0.5, new[:, :], ALU.mult, ALU.add)\
                            .then_inc(cell_ready, 1)
                        dve.wait_ge(tanh_ready, n)
                        dve.scalar_tensor_tensor(hs[:, bass.ds(t + j, 1), :].rearrange("p a b -> p (a b)"),
                                                 gates[:, O_, :], 1.0, tanh_c[:, :],
                                                 ALU.add, ALU.mult).then_inc(h_ready, 1)
                quads(dve, body)

        h4, agg4 = sb("h4", [P, 2, G, P]), sb("agg4", [P, 2, G, P])
        lw, act_out, r3, y = (sb(n, [P, 2, G, P]) for n in ("lw", "act_out", "r3", "y"))
        stats, mv = sb("stats", [P, G, 6]), sb("mv", [P, G, 2])
        veps, rstd, minus_half = sb("veps", [P, G]), sb("rstd", [P, G]), sb("minus_half", [P, G])
        hdinv = sb("hdinv", [P, B])
        names = ("h4_ready agg4_ready lwt_p lw_ready o_p act_ready r3_ready st_ready mv_ready veps_ready rstd_ready "
                 "y_ready consts").split()
        s = {n: sem(n) for n in names}
        stored = [sem(f"stored{i}") for i in range(2)]
        lwt_b = [c0.enter_context(nc.psum_tensor(f"r_lwt{i}", [P, G, P], F32)) for i in range(2)]
        o_b = [c0.enter_context(nc.psum_tensor(f"r_o{i}", [P, G, P], F32)) for i in range(2)]
        NGR = B // G

        def schedule(eng, body):
            pairs(eng, (0,), (1, NGR // 2), (NGR // 2,), body)

        def steps(pair):
            for i in range(2):
                g = Steps(pair, i, 2, NGR)
                yield g, g.has(0), g.has(-1)

        def w(eng, name, g, d=0):
            eng.wait_ge(s[name], g.at(d) + 1)

        def after(eng, name, g, d):
            if not g.static or g.at(d) >= 0:
                eng.wait_ge(s[name], min(g.at(d), NGR - 1) + 1 if g.static else g.at(d) + 1)

        with ExitStack() as c1:
            block = c1.enter_context(nc.Block())

            @block.sync
            def _(sp):
                def body(pair):
                    for g, one, two in steps(pair):
                        if two:
                            q = g.mod(2, -1)
                            w(sp, "y_ready", g, -1)
                            sp.sem_inc(held["SP"], 1)
                            sp.dma_start(out[bass.ds(g.at(-1) * G, G), :, :].rearrange("b i d -> i b d"),
                                         y[:, q, :, :]).then_inc(stored[q], 16)
                schedule(sp, body)
                for q in range(2):
                    sp.wait_ge(stored[q], 16 * (NGR // 2))

            @block.gpsimd
            def _(pool):
                pool.memset(minus_half[:, :], -0.5).then_inc(s["consts"], 1)
                pool.wait_ge(s["consts"], 1)

                def body(pair):
                    for g, one, two in steps(pair):
                        if one:
                            after(pool, "o_p", g, -2)
                            pool.sem_inc(held["Pool"], 1)
                            pool.tensor_copy(agg4[:, g.mod(2), :, :], agg[:, bass.ds(g.at() * G, G), :])\
                                .then_inc(s["agg4_ready"], 1)
                            after(pool, "lwt_p", g, -2)
                            pool.sem_inc(held["Pool"], 1)
                            pool.tensor_copy(h4[:, g.mod(2), :, :],
                                             hs[:, :, bass.ds(g.at() * G, G)].rearrange("p t b -> p b t"))\
                                .then_inc(s["h4_ready"], 1)
                        if two:
                            w(pool, "mv_ready", g, -1)
                            pool.sem_inc(held["Pool"], 1)
                            pool.tensor_scalar(veps[:, :], mv[:, :, 1], EPS, None, ALU.add)\
                                .then_inc(s["veps_ready"], 1)
                            w(pool, "veps_ready", g, -1)
                            pool.tensor_tensor(rstd[:, :], veps[:, :], minus_half[:, :], ALU.pow)\
                                .then_inc(s["rstd_ready"], 1)
                schedule(pool, body)

            @block.tensor
            def _(pe):
                def body(pair):
                    for g, one, two in steps(pair):
                        q = g.mod(2)
                        if one:
                            w(pe, "h4_ready", g)
                            after(pe, "lw_ready", g, -2)
                            for j in range(G):
                                last = pe.transpose(lwt_b[q][:, j, :], h4[:, q, j, :], ident[:, :])
                            last.then_inc(s["lwt_p"], 1)
                        if two:
                            q = g.mod(2, -1)
                            w(pe, "lw_ready", g, -1)
                            w(pe, "agg4_ready", g, -1)
                            after(pe, "act_ready", g, -3)
                            for j in range(G):
                                last = pe.matmul(o_b[q][:, j, :], agg4[:, q, j, :], lw[:, q, j, :],
                                                 start=True, stop=True)
                            last.then_inc(s["o_p"], 1)
                schedule(pe, body)

            @block.scalar
            def _(act):
                def body(pair):
                    for g, one, two in steps(pair):
                        if one:
                            q = g.mod(2)
                            w(act, "lwt_p", g)
                            after(act, "o_p", g, -2)
                            act.activation(lw[:, q, :, :], lwt_b[q][:, :, :], ACT.Copy, scale=0.5)\
                                .then_inc(s["lw_ready"], 1)
                        if two:
                            q = g.mod(2, -1)
                            w(act, "o_p", g, -1)
                            after(act, "r3_ready", g, -3)
                            for j in range(G):
                                last = act.activation(act_out[:, q, j, :], o_b[q][:, j, :], ACT.Sigmoid,
                                                      scale=dinv[:, bass.ds(g.at(-1) * G + j, 1)])
                            last.then_inc(s["act_ready"], 1)
                schedule(act, body)

            @block.vector
            def _(dve):
                def body(pair):
                    for g, one, two in steps(pair):
                        if two:
                            q = g.mod(2, -1)
                            w(dve, "act_ready", g, -1)
                            after(dve, "y_ready", g, -3)
                            dve.tensor_tensor(r3[:, q, :, :], act_out[:, q, :, :],
                                              xres[:, bass.ds(g.at(-1) * G, G), :], ALU.add)\
                                .then_inc(s["r3_ready"], 1)
                            w(dve, "r3_ready", g, -1)
                            after(dve, "mv_ready", g, -2)
                            for j in range(G):
                                last = dve.bn_stats(stats[:, j, :], r3[:, q, j, :])
                            last.then_inc(s["st_ready"], 1)
                            w(dve, "st_ready", g, -1)
                            after(dve, "rstd_ready", g, -2)
                            after(dve, "y_ready", g, -2)
                            dve.sem_inc(held["DVE"], 1)
                            for j in range(G):
                                last = dve.bn_aggr(mv[:, j, :], stats[:, j, :])
                            last.then_inc(s["mv_ready"], 1)
                            w(dve, "rstd_ready", g, -1)
                            if g.static and g.at(-1) < 2:
                                pass
                            else:
                                dve.wait_ge(stored[q], g.pair * 16 + 16 * ((g.inner - 1) // 2))
                            for j in range(G):
                                last = dve.tensor_scalar(y[:, q, j, :], r3[:, q, j, :], mv[:, j, 0:1],
                                                         rstd[:, j:j + 1], ALU.subtract, ALU.mult)
                            last.then_inc(s["y_ready"], 1)
                schedule(dve, body)


def lay_out(i):
    c = np.ascontiguousarray
    x, adj = np.asarray(i["x"]), np.asarray(i["adj"])
    offsets, _ = gaussian_constants()
    cols = np.zeros((B, P, ALL_UNITS * R), np.float32)
    cols[:, :, :P] = adj
    L0, L1, L2, L3 = "L0_gnn_", "L1_gnn_", "L2_gnn_", "L3_gnn_"
    g = {n: np.asarray(v) for n, v in i.items()}
    return {
        "x_rows": c(x.transpose(1, 0, 2)),
        "x_cols": c(x.transpose(2, 0, 1)),
        "adj_rows": c(adj.transpose(1, 0, 2)),
        "adj_t": c(adj.transpose(2, 0, 1)),
        "adj_cols": c(cols.reshape(B, P, ALL_UNITS, R).transpose(0, 2, 1, 3)),
        "offsets": c(offsets.reshape(NG, 1)),
        "mask_rows": c(g["nodemask"].T),
        "w1t": c(g[L0 + "W1"].T), "w2t": c(g[L0 + "W2"].T), "wat": c(g[L0 + "Wa"].T),
        "wd1t": c(g[L0 + "Wd1"].T), "wd2t": c(g[L0 + "Wd2"].T),
        "b1c": c(g[L0 + "b1"].reshape(P, 1)), "bd1c": c(g[L0 + "bd1"].reshape(P, 1)),
        "b2row": c(g[L0 + "b2"].reshape(1, P)), "bd2row": c(g[L0 + "bd2"].reshape(1, P)),
        "wq": c(g[L1 + "Wq"]), "wqt": c(g[L1 + "Wq"].T), "wkt": c(g[L1 + "Wk"].T), "wv": c(g[L1 + "Wv"]),
        "gamma_row": c(g[L1 + "gamma"].reshape(1, P)), "beta_row": c(g[L1 + "beta"].reshape(1, P)),
        "w_layer": c(g[L2 + "W_layer"]), "w_layer_t": c(g[L2 + "W_layer"].T),
        "w_self": c(g[L2 + "W_att_self"]), "w_neigh": c(g[L2 + "W_att_neighbor"]),
        "b_layer_row": c(g[L2 + "b_layer"].reshape(1, P)),
        "conv_wt": c(g[L3 + "conv_w"].transpose(1, 2, 0)), "conv_b_row": c(g[L3 + "conv_b"].reshape(1, P)),
        "w_iht": c(g[L3 + "w_ih"].T), "w_hht": c(g[L3 + "w_hh"].T),
        "b_ih_row": c(g[L3 + "b_ih"].reshape(1, 4 * P)), "b_hh_row": c(g[L3 + "b_hh"].reshape(1, 4 * P)),
    }


def kernel(**inputs):
    import concourse.bacc as bacc
    from concourse.bass_utils import run_bass_kernel_spmd

    nc = bacc.Bacc("TRN2", target_bir_lowering=False, num_devices=1)
    arrays = lay_out(inputs)
    aps = {n: nc.dram_tensor(f"in_{n}", v.shape, mybir.dt.from_np(v.dtype), kind="ExternalInput").ap()
           for n, v in arrays.items()}
    out = nc.dram_tensor("out", (B, P, P), F32, kind="ExternalOutput").ap()
    build(nc, aps, out)
    r = run_bass_kernel_spmd(nc, [{f"in_{n}": v for n, v in arrays.items()}], core_ids=[0])
    return r.results[0]["out"]
```

```python
from contextlib import ExitStack

import numpy as np
import concourse.bass as bass
from concourse import mybir

ALU = mybir.AluOpType
ACT = mybir.ActivationFunctionType
AX = mybir.AxisListType
F32 = mybir.dt.float32
BF16 = mybir.dt.bfloat16
U32 = mybir.dt.uint32
I32 = mybir.dt.int32

P = 128
B = 64
NG = 64
CUTOFF = 5.0
R = 6
UNIT = R * P
HALF = UNIT // 2
DIRECT = 2 * R - 1
RANKS = 24
OVER = RANKS - DIRECT
ALL_UNITS = -(-P // R)
UNIT_BUFS = 4
CLAMP = 40.0
LN2 = float(np.log(2.0))
EPS = 1e-5
G = 4


def gaussian_constants():
    offsets = np.linspace(0.0, CUTOFF, NG, dtype=np.float32)
    width = np.float32(offsets[1] - offsets[0])
    return offsets, float(np.float32(-0.5) / (width * width))


class Steps:

    def __init__(self, pair, inner, per_pair, total):
        self.pair, self.inner, self.per_pair, self.total = pair, inner, per_pair, total
        self.static = isinstance(pair, int)

    def has(self, d=0):
        return not self.static or 0 <= self.pair * self.per_pair + self.inner + d < self.total

    def at(self, d=0):
        return self.pair * self.per_pair + (self.inner + d)

    def mod(self, n, d=0):
        return (self.inner + d) % n


def pairs(eng, first, loop, last, body):
    for pair in first:
        body(pair)
    with eng.Fori(loop[0], loop[1]) as pair:
        body(pair)
    for pair in last:
        body(pair)


def build(nc, a, out):
    offsets, coeff = gaussian_constants()
    ctx = ExitStack()
    with ctx:
        def sb(name, shape, dt=F32):
            return ctx.enter_context(nc.sbuf_tensor(name, shape, dt))

        xin = sb("xin", [P, B, P])
        xres = sb("xres", [P, B, P])
        ident = sb("ident", [P, P])
        iota_row = sb("iota_row", [P, P])
        iota_col = sb("iota_col", [P, 1])
        flag = sb("flag", [1, 1], I32)
        deg = sb("deg", [P, 2, G])
        edge_val = nc.dram_tensor("edge_val", [B, 2, P, R], F32, kind="Internal").ap()
        edge_idx = nc.dram_tensor("edge_idx", [B, 2, P, R], BF16, kind="Internal").ap()
        all_idx = nc.dram_tensor("all_idx", [ALL_UNITS, P * R], BF16, kind="Internal").ap()

        held = {n: ctx.enter_context(nc.semaphore("held_" + n)) for n in ("SP", "DVE", "Pool")}

        k = dict(locals())
        k["phase_semaphores"] = []
        constants_block(nc, k)
        with ExitStack() as c0:
            k["c0"] = c0
            layer0(nc, a, k)
            clear_semaphores(nc, k)
        k["dyn"] = sb("dyn", [P, P, B])
        k["agg"] = sb("agg", [P, B, P])
        k["dinv"] = sb("dinv", [P, B])
        layers12(nc, a, k)
        lstm(nc, a, k)


def phase_semaphore(nc, stack, k, name):
    handle = stack.enter_context(nc.semaphore(name))
    k["phase_semaphores"].append(handle)
    return handle


def clear_semaphores(nc, k):
    with ExitStack() as c:
        block = c.enter_context(nc.Block())

        @block.sync
        def _(sp):
            for handle in k["phase_semaphores"]:
                sp.sem_clear(handle)
    k["phase_semaphores"].clear()


def constants_block(nc, k):
    with ExitStack() as c:
        iota_done, cast_done, all_idx_stored = (k["ctx"].enter_context(nc.semaphore(n))
                                                for n in ("iota_done", "cast_done", "all_idx_stored"))
        columns = c.enter_context(nc.sbuf_tensor("columns", [ALL_UNITS, P * R], F32))
        columns16 = c.enter_context(nc.sbuf_tensor("columns16", [ALL_UNITS, P * R], BF16))
        block = c.enter_context(nc.Block())

        @block.gpsimd
        def _(pool):
            pool.iota(k["iota_row"][:, :], pattern=[[1, P]], base=0, channel_multiplier=0,
                      allow_small_or_imprecise_dtypes=True).then_inc(iota_done, 1)
            pool.iota(k["iota_col"][:, :], pattern=[[0, 1]], base=0, channel_multiplier=1,
                      allow_small_or_imprecise_dtypes=True).then_inc(iota_done, 1)
            pool.iota(columns[:, :].rearrange("u (i r) -> u i r", r=R), pattern=[[0, P], [1, R]], base=0,
                      channel_multiplier=R, allow_small_or_imprecise_dtypes=True).then_inc(iota_done, 1)

        @block.vector
        def _(dve):
            dve.wait_ge(iota_done, 2)
            dve.tensor_scalar(k["ident"][:, :], k["iota_row"][:, :], k["iota_col"][:, :], None, ALU.is_equal)
            dve.wait_ge(iota_done, 3)
            dve.tensor_copy(columns16[:, :], columns[:, :]).then_inc(cast_done, 1)

        @block.sync
        def _(sp):
            sp.wait_ge(cast_done, 1)
            sp.dma_start(k["all_idx"], columns16[:, :]).then_inc(all_idx_stored, 16)
            sp.wait_ge(all_idx_stored, 16)


def layer0(nc, a, k):
    c0 = k["c0"]
    offsets, coeff = gaussian_constants()
    xin, xres, ident, iota_row, iota_col, flag = (k[n] for n in ("xin", "xres", "ident", "iota_row", "iota_col", "flag"))
    edge_val, edge_idx = k["edge_val"], k["edge_idx"]

    def sb(name, shape, dt=F32):
        return c0.enter_context(nc.sbuf_tensor(name, shape, dt))

    def ps(name, shape, dt=F32):
        return c0.enter_context(nc.psum_tensor(name, shape, dt))

    def sem(name):
        return phase_semaphore(nc, c0, k, name)

    w1t = sb("w1t", [P, P])
    w2t = sb("w2t", [P, P])
    wat = sb("wat", [P, P])
    wd1t = sb("wd1t", [P, P])
    wd2t = sb("wd2t", [P, P])
    b1c = sb("b1c", [P, 1])
    bd1c = sb("bd1c", [P, 1])
    off_c = sb("off_c", [P, 1])
    noff_c = sb("noff_c", [P, 1])
    b2row = sb("b2row", [1, P])
    bd2row = sb("bd2row", [1, P])
    ones_row = sb("ones_row", [1, P])
    mln2 = sb("mln2", [P, P])
    before = sb("before", [P, P])
    b2bc = sb("b2bc", [P, P])
    bd2bc = sb("bd2bc", [P, P])
    adj_w = sb("adj_w", [P, 2, P])
    adj_r1 = sb("adj_r1", [P, P])
    adj_r2 = sb("adj_r2", [P, P])
    found = sb("found", [P, 2 * RANKS + 2])
    found_idx = sb("found_idx", [P, RANKS], U32)
    over_bits = sb("over_bits", [P, OVER])
    over_cnt = sb("over_cnt", [P, 1])
    slot_from = sb("slot_from", [P, P])
    slot_of = sb("slot_of", [P, P])
    rank_hit = sb("rank_hit", [P, OVER])
    over_pick = sb("over_pick", [P, 2, OVER])
    ev = sb("ev", [P, 2, 2 * R])
    ei = sb("ei", [P, 2, 2 * R])
    ei16 = sb("ei16", [P, 2, 2 * R], BF16)
    over_row = sb("over_row", [P, B])
    over_end = sb("over_end", [P, B])
    last_rank = sb("last_rank", [P, B])
    least = sb("least", [P, B])
    over_t = sb("over_t", [P, 2, P])
    val_bc = sb("val_bc", [P, UNIT_BUFS, HALF])
    idx_bc = sb("idx_bc", [P, UNIT_BUFS, UNIT], BF16)
    val_own = sb("val_own", [P, UNIT_BUFS, R])
    val_sq = sb("val_sq", [P, UNIT_BUFS, R])
    dist2 = sb("dist2", [P, HALF])
    gauss = sb("gauss", [P, 2, HALF])
    pick = sb("pick", [P, 2, UNIT], BF16)
    absz = sb("absz", [P, UNIT])
    relz = sb("relz", [P, UNIT])
    expd = sb("expd", [P, UNIT])
    logd = sb("logd", [P, UNIT])
    hid = sb("hid", [P, 2, UNIT])
    rfe = sb("rfe", [P, 2, UNIT])
    msg = sb("msg", [P, 2, UNIT])
    sum1, sum2, sum3 = sb("sum1", [P, 2 * P]), sb("sum2", [P, P]), sb("sum3", [P, 2, P])
    xt_w = sb("xt_w", [P, 2, P])
    adjt_w = sb("adjt_w", [P, 2, P])
    adjt_sq = sb("adjt_sq", [P, 2, P])
    rf_hi = sb("rf_hi", [P, 2, P], BF16)
    rf_mid = sb("rf_mid", [P, 2, P], BF16)
    rf_lo = sb("rf_lo", [P, 2, P], BF16)
    rf32 = sb("rf32", [P, P])
    rf_r1 = sb("rf_r1", [P, P])
    rfb = sb("rfb", [P, 2, P])
    xb = sb("xb", [P, 2, P])
    yt = sb("yt", [P, P])
    t_u = sb("t_u", [P, P])
    t_cl = sb("t_cl", [P, P])
    t_ex = sb("t_ex", [P, P])
    t_lg = sb("t_lg", [P, P])
    t_h = sb("t_h", [P, P])
    v0 = sb("v0", [P, 4])

    zb = ps("zb", [P, 2, 512])
    wf = ps("wf", [P, 2, 512])
    rg = ps("rg", [P, 2, 512])
    yp = ps("yp", [P, 512])
    mb = ps("mb", [P, 512])
    p_out = rg[:, 0, HALF:512]
    p_u = rg[:, 1, HALF:512]
    p_rf = mb[:, 0:P]
    p_over = mb[:, P:P + 2 * RANKS + 2]
    p_start = mb[:, 200:201]
    p_flag = mb[0:1, 201:202]

    def column(bank_pair, r):
        return bank_pair[:, r // 3, r % 3 * P:(r % 3 + 1) * P]

    weights_in = sem("weights_in")
    x_in = sem("x_in")
    adj_in = [sem(f"adj_in{i}") for i in range(2)]
    xt_in = [sem(f"xt_in{i}") for i in range(2)]
    adjt_in = [sem(f"adjt_in{i}") for i in range(2)]
    edges_stored = sem("edges_stored")
    unit_in = [sem(f"unit_in{i}") for i in range(UNIT_BUFS)]
    names = (
        "consts_ready bias_ready bias_read memsets_done "
        "top1 top2 top3 rest1 rest2 idx3 idxf cnt start_ready start_copied from_ready slot_ready over_gathered "
        "hits_ready picks_ready edges16 adj_read "
        "dist2_ready gauss_ready z_ready abs_ready relu_ready exp_ready log_ready hid_ready pick_ready valsq_ready "
        "rg_ready rfe_ready wf_ready msg_ready sum1_ready sum2_ready sum3_ready summed "
        "rf_ready rfhi_ready rfr1_ready rfmid_ready rflo_ready rfb_ready adjtsq_ready xb_ready yt_ready u_ready "
        "u_read uclamped_ready uexp_ready ulog_ready uh_ready out_ready res_ready over_t_ready"
    ).split()
    s = {n: sem("l0_" + n) for n in names}

    n_weights = 12

    with ExitStack() as c1:
        block = c1.enter_context(nc.Block())

        @block.sync
        def _(sp):
            for half in range(2):
                sp.dma_start(w1t[half * NG:(half + 1) * NG, :], a["w1t"]).then_inc(weights_in, 16)
                sp.dma_start(off_c[half * NG:(half + 1) * NG, :], a["offsets"]).then_inc(weights_in, 16)
            for dst, src in ((w2t, "w2t"), (wat, "wat"), (wd1t, "wd1t"), (wd2t, "wd2t"), (b1c, "b1c"),
                             (bd1c, "bd1c"), (b2row, "b2row"), (bd2row, "bd2row")):
                sp.dma_start(dst[:, :], a[src]).then_inc(weights_in, 16)

        @block.vector
        def _(dve):
            dve.memset(mln2[:, :], -LN2)
            dve.memset(ones_row[:, :], 1.0)
            dve.memset(over_row[:, :], 0.0)
            dve.tensor_scalar(before[:, :], iota_row[:, :], iota_col[:, :], None, ALU.is_gt)
            dve.tensor_copy(found[:, 2 * RANKS + 1:], iota_col[:, :]).then_inc(s["consts_ready"], 1)
            dve.wait_ge(weights_in, 16 * n_weights)
            dve.tensor_scalar(noff_c[:, :], off_c[:, :], -1.0, None, ALU.mult)
            dve.wait_ge(s["bias_ready"], 1)
            dve.tensor_copy(b2bc[:, :], p_rf)
            dve.tensor_copy(bd2bc[:, :], p_u)

        @block.tensor
        def _(pe):
            pe.wait_ge(weights_in, 16 * n_weights)
            pe.wait_ge(s["consts_ready"], 1)
            pe.matmul(p_rf, mln2[:, :], w2t[:, :], start=True, stop=False)
            pe.matmul(p_rf, ones_row[:, :], b2row[:, :], start=False, stop=True)
            pe.matmul(p_u, mln2[:, :], wd2t[:, :], start=True, stop=False)
            pe.matmul(p_u, ones_row[:, :], bd2row[:, :], start=False, stop=True).then_inc(s["bias_ready"], 1)

    def run(block, dense):
        per_graph = ALL_UNITS if dense else 2
        per_pair = 2 * per_graph
        nu, ng = per_graph * B, B
        u0 = 2 * B if dense else 0
        g0 = B if dense else 0
        val_src = a["adj_cols"] if dense else edge_val
        idx_src = k["all_idx"] if dense else edge_idx

        def unit(pair, i):
            return Steps(pair, i, per_pair, nu)

        def graph(pair, i):
            return Steps(pair, i // per_graph, 2, ng)

        def unit_count(u, d, q):
            before_pair = per_pair // UNIT_BUFS
            return u.pair * (64 * before_pair) + 64 * ((u.inner + d) // UNIT_BUFS + 1 + u0 // UNIT_BUFS)

        def adj_count(g, q, d=0):
            return g.pair * 16 + 16 * ((g.inner + d) // 2 + 1 + g0 // 2)

        def schedule(eng, body):
            if dense:
                pairs(eng, (-1, 0), (1, B // 2 - 1), (B // 2 - 1, B // 2), body)
            else:
                pairs(eng, (-2, -1, 0), (1, B // 2 - 2), (B // 2 - 2, B // 2 - 1, B // 2), body)

        def w(eng, name, value):
            eng.wait_ge(s[name], value)

        def after(eng, name, st, d, start):
            i = min(st.at(d), st.total - 1) if st.static else st.at(d)
            if not st.static or i + start >= 0:
                eng.wait_ge(s[name], i + start + 1)

        def after_graph(eng, g, d, name="summed"):
            if not g.static or g.at(d) + g0 >= 0:
                eng.wait_ge(s[name], (g.at(d) + 1) * per_graph + u0 if not g.static or g.at(d) >= 0
                            else 2 * (g.at(d) + g0 + 1))

        def alone(eng):
            eng.sem_inc(k["held"][eng.engine.name], 1)

        @block.sync
        def _(sp):
            if not dense:
                for c in range(4):
                    sp.dma_start(xin[:, c * (B // 4):(c + 1) * (B // 4), :],
                                 a["x_rows"][:, c * (B // 4):(c + 1) * (B // 4), :]).then_inc(x_in, 16)

            def load_unit(u, d, g, dg, kk):
                q = u.mod(UNIT_BUFS, d)
                after(sp, "dist2_ready", u, d - UNIT_BUFS, u0)
                after(sp, "pick_ready", u, d - UNIT_BUFS, u0)
                after(sp, "valsq_ready", u, d - UNIT_BUFS, u0)
                alone(sp)
                lo, hi = slice(0, NG), slice(NG, P)
                gi = g.at(dg)
                for half, part in ((0, lo), (1, hi)):
                    sp.dma_start(val_bc[part, q, :],
                                 val_src[bass.ds(gi, 1), kk, half * NG:(half + 1) * NG, :]
                                 .rearrange("a i r -> a (i r)").broadcast_to((NG, HALF))).then_inc(unit_in[q], 16)
                if dense:
                    isrc = idx_src[kk:kk + 1, :].broadcast_to((P, UNIT))
                else:
                    isrc = idx_src[bass.ds(gi, 1), kk, :, :].rearrange("a i r -> a (i r)").broadcast_to((P, UNIT))
                sp.dma_start(idx_bc[:, q, :], isrc).then_inc(unit_in[q], 16)
                sp.dma_start(val_own[:, q, :],
                             val_src[bass.ds(gi, 1), kk, :, :].rearrange("a i r -> (a i) r")).then_inc(unit_in[q], 16)

            def body(pair):
                for i in range(per_pair):
                    u, g = unit(pair, i), graph(pair, i)
                    if i % per_graph == 0:
                        if not dense and g.has(4):
                            after(sp, "adj_read", g, 2, 0)
                            alone(sp)
                            sp.dma_start(adj_w[:, g.mod(2, 4), :], a["adj_rows"][:, g.at(4), :])\
                                .then_inc(adj_in[g.mod(2, 4)], 16)
                        if g.has(2):
                            after(sp, "rf_ready", g, 0, g0)
                            alone(sp)
                            sp.dma_start(xt_w[:, g.mod(2, 2), :], a["x_cols"][:, g.at(2), :])\
                                .then_inc(xt_in[g.mod(2, 2)], 16)
                        if g.has(1):
                            after(sp, "adjtsq_ready", g, -1, g0)
                            alone(sp)
                            sp.dma_start(adjt_w[:, g.mod(2, 1), :], a["adj_t"][:, g.at(1), :])\
                                .then_inc(adjt_in[g.mod(2, 1)], 16)
                    if not dense and i % 2 == 0 and g.has(2):
                        w(sp, "edges16", g.at(2) + 1)
                        alone(sp)
                        q = g.mod(2, 2)
                        sp.dma_start(edge_val[bass.ds(g.at(2), 1), :, :, :].rearrange("a h i r -> (a i) h r"),
                                     ev[:, q, :].rearrange("p (h r) -> p h r", h=2)).then_inc(edges_stored, 16)
                        sp.dma_start(edge_idx[bass.ds(g.at(2), 1), :, :, :].rearrange("a h i r -> (a i) h r"),
                                     ei16[:, q, :].rearrange("p (h r) -> p h r", h=2)).then_inc(edges_stored, 16)
                        sp.wait_ge(edges_stored, 32 * (g.at(2) + 1))
                        alone(sp)
                        for kk in range(2):
                            load_unit(u, 4 + kk, g, 2, kk)
                    if dense and u.has(3):
                        kk = (i + 3) % per_graph
                        load_unit(u, 3, g, (i + 3) // per_graph - i // per_graph, kk)
            schedule(sp, body)
            if not dense:
                sp.wait_ge(x_in, 64)

        @block.gpsimd
        def _(pool):
            if not dense:
                pool.wait_ge(x_in, 64)

            def body(pair):
                for i in range(per_pair):
                    u, g = unit(pair, i), graph(pair, i)
                    if u.has(1):
                        q = u.mod(UNIT_BUFS, 1)
                        pool.wait_ge(unit_in[q], unit_count(u, 1, q))
                        after(pool, "msg_ready", u, 1 - UNIT_BUFS, u0)
                        pool.tensor_tensor(val_sq[:, q, :], val_own[:, q, :], val_own[:, q, :], ALU.mult)\
                            .then_inc(s["valsq_ready"], 1)
                    if i % per_graph == 0 and g.has(0):
                        q = g.mod(2)
                        pool.wait_ge(adjt_in[q], adj_count(g, q))
                        after_graph(pool, g, -2)
                        pool.tensor_tensor(adjt_sq[:, q, :], adjt_w[:, q, :], adjt_w[:, q, :], ALU.mult)\
                            .then_inc(s["adjtsq_ready"], 1)
                        after(pool, "res_ready", g, -2, g0)
                        pool.tensor_tensor(xb[:, q, :], xin[:, g.at(), :], bd2bc[:, :], ALU.add)\
                            .then_inc(s["xb_ready"], 1)
                    if i % per_graph == 0 and g.has(1):
                        w(pool, "rfhi_ready", g.at(1) + g0 + 1)
                        after_graph(pool, g, -1)
                        after(pool, "rflo_ready", g, 0, g0)
                        pool.tensor_tensor(rf_r1[:, :], rf32[:, :], rf_hi[:, g.mod(2, 1), :], ALU.subtract)\
                            .then_inc(s["rfr1_ready"], 1)
                        pool.tensor_tensor(rfb[:, g.mod(2, 1), :], rf32[:, :], b2bc[:, :], ALU.mult)\
                            .then_inc(s["rfb_ready"], 1)
                        w(pool, "rfr1_ready", g.at(1) + g0 + 1)
                        alone(pool)
                        pool.tensor_copy(rf_mid[:, g.mod(2, 1), :], rf_r1[:, :]).then_inc(s["rfmid_ready"], 1)
                        w(pool, "rfmid_ready", g.at(1) + g0 + 1)
                        pool.tensor_tensor(rf_lo[:, g.mod(2, 1), :], rf_r1[:, :], rf_mid[:, g.mod(2, 1), :],
                                           ALU.subtract).then_inc(s["rflo_ready"], 1)
                    if u.has(0):
                        q = u.mod(2)
                        w(pool, "msg_ready", u.at() + u0 + 1)
                        after(pool, "sum2_ready", u, -1, u0)
                        pool.tensor_tensor(sum1[:, :], msg[:, q, 0:2 * P], msg[:, q, 2 * P:4 * P], ALU.add)\
                            .then_inc(s["sum1_ready"], 1)
                        w(pool, "sum1_ready", u.at() + u0 + 1)
                        after(pool, "sum3_ready", u, -1, u0)
                        pool.tensor_tensor(sum2[:, :], sum1[:, 0:P], sum1[:, P:2 * P], ALU.add)\
                            .then_inc(s["sum2_ready"], 1)
                        w(pool, "sum2_ready", u.at() + u0 + 1)
                        after(pool, "summed", u, -2, u0)
                        pool.tensor_tensor(sum3[:, q, :], sum2[:, :], msg[:, q, 4 * P:5 * P], ALU.add)\
                            .then_inc(s["sum3_ready"], 1)
            schedule(pool, body)

        @block.scalar
        def _(act):
            if not dense:
                act.preload_act_table_set("natural_log_exp_and_others")

            def body(pair):
                for i in range(per_pair):
                    u, g = unit(pair, i), graph(pair, i)
                    k_in = i % per_graph
                    if u.has(0):
                        q = u.mod(2)
                        w(act, "rg_ready", u.at() + u0 + 1)
                        after(act, "msg_ready", u, -2, u0)
                        act.activation(rfe[:, q, :].rearrange("p (a n) -> p a n", a=2), rg[:, :, 0:HALF], ACT.Copy).then_inc(s["rfe_ready"], 1)
                    if u.has(2):
                        q = u.mod(UNIT_BUFS, 2)
                        act.wait_ge(unit_in[q], unit_count(u, 2, q))
                        after(act, "gauss_ready", u, 1, u0)
                        act.activation(dist2[:, :], val_bc[:, q, :], ACT.Square, bias=noff_c[:, :])\
                            .then_inc(s["dist2_ready"], 1)
                        w(act, "dist2_ready", u.at(2) + u0 + 1)
                        after(act, "z_ready", u, 0, u0)
                        act.activation(gauss[:, u.mod(2, 2), :], dist2[:, :], ACT.Exp, scale=coeff)\
                            .then_inc(s["gauss_ready"], 1)
                    if k_in == 1 and g.has(-1):
                        after_graph(act, g, -1)
                        after(act, "u_ready", g, -2, g0)
                        act.activation(yt[:, :], yp[:, 0:P], ACT.Copy).then_inc(s["yt_ready"], 1)
                    if u.has(1):
                        w(act, "z_ready", u.at(1) + u0 + 1)
                        after(act, "exp_ready", u, 0, u0)
                        after(act, "hid_ready", u, 0, u0)
                        act.activation(absz[:, :].rearrange("p (a n) -> p a n", a=2), zb[:, :, 0:HALF], ACT.Abs,
                                       bias=b1c[:, :]).then_inc(s["abs_ready"], 1)
                        act.activation(relz[:, :].rearrange("p (a n) -> p a n", a=2), zb[:, :, 0:HALF], ACT.Relu,
                                       bias=b1c[:, :]).then_inc(s["relu_ready"], 1)
                        w(act, "abs_ready", u.at(1) + u0 + 1)
                        after(act, "log_ready", u, 0, u0)
                        act.activation(expd[:, :], absz[:, :], ACT.Exp, scale=-1.0).then_inc(s["exp_ready"], 1)
                        w(act, "exp_ready", u.at(1) + u0 + 1)
                        act.activation(logd[:, :], expd[:, :], ACT.Ln, bias=1.0).then_inc(s["log_ready"], 1)
                    if k_in == 0 and g.has(1):
                        w(act, "rf_ready", g.at(1) + g0 + 1)
                        after_graph(act, g, -1, "rg_ready")
                        after(act, "rfb_ready", g, 0, g0)
                        act.activation(rf32[:, :], p_rf, ACT.Copy)
                        act.activation(rf_hi[:, g.mod(2, 1), :], p_rf, ACT.Copy).then_inc(s["rfhi_ready"], 1)
                    if k_in == 0 and g.has(-2):
                        w(act, "uclamped_ready", g.at(-2) + g0 + 1)
                        after(act, "ulog_ready", g, -3, g0)
                        act.activation(t_ex[:, :], t_cl[:, :], ACT.Exp).then_inc(s["uexp_ready"], 1)
                        w(act, "uexp_ready", g.at(-2) + g0 + 1)
                        after(act, "uh_ready", g, -3, g0)
                        act.activation(t_lg[:, :], t_ex[:, :], ACT.Ln, bias=1.0).then_inc(s["ulog_ready"], 1)
            schedule(act, body)

        @block.tensor
        def _(pe):
            def body(pair):
                for i in range(per_pair):
                    u, g = unit(pair, i), graph(pair, i)
                    k_in = i % per_graph
                    q = u.mod(2)
                    if u.has(1):
                        qn = u.mod(2, 1)
                        w(pe, "gauss_ready", u.at(1) + u0 + 1)
                        after(pe, "relu_ready", u, 0, u0)
                        pe.matmul(zb[:, 0, 0:HALF], w1t[0:NG, :], gauss[0:NG, qn, :], start=True, stop=True)
                        pe.matmul(zb[:, 1, 0:HALF], w1t[NG:P, :], gauss[NG:P, qn, :], start=True, stop=True)\
                            .then_inc(s["z_ready"], 1)
                    if k_in == 1 and g.has(-1):
                        w(pe, "yt_ready", g.at(-1) + g0 + 1)
                        after(pe, "rfe_ready", u, 0, u0)
                        pe.matmul(p_u, wd1t[:, :], yt[:, :], start=True, stop=True).then_inc(s["u_ready"], 1)
                    if k_in == 1 and g.has(-2):
                        w(pe, "uh_ready", g.at(-2) + g0 + 1)
                        after(pe, "rfe_ready", u, 0, u0)
                        pe.matmul(p_out, t_h[:, :], wd2t[:, :], start=True, stop=True).then_inc(s["out_ready"], 1)
                    if u.has(0):
                        w(pe, "hid_ready", u.at() + u0 + 1)
                        after(pe, "msg_ready", u, -1, u0)
                        h = hid[:, q, :].rearrange("p (i r) -> p r i", r=R)
                        for r in range(R):
                            last = pe.matmul(column(wf, r), h[:, r, :], w2t[:, :], start=True, stop=True)
                        last.then_inc(s["wf_ready"], 1)
                    if u.has(1):
                        gn, kn = Steps(g.pair, (i + 1) // per_graph, 2, ng), (i + 1) % per_graph
                        w(pe, "pick_ready", u.at(1) + u0 + 1)
                        after(pe, "rfe_ready", u, 0, u0)
                        if kn == 0:
                            w(pe, "rflo_ready", gn.at() + g0 + 1)
                        if k_in == 1 and g.has(-1):
                            w(pe, "u_read", g.at(-1) + g0 + 1)
                        if k_in == 1 and g.has(-2):
                            w(pe, "res_ready", g.at(-2) + g0 + 1)
                        picked = pick[:, u.mod(2, 1), :].rearrange("p (i r) -> p r i", r=R)
                        for r in range(R):
                            for part in (rf_hi, rf_mid, rf_lo):
                                last = pe.matmul(column(rg, r), picked[:, r, :], part[:, gn.mod(2), :],
                                                 start=part is rf_hi, stop=part is rf_lo)
                        last.then_inc(s["rg_ready"], 1)
                    if k_in == 0 and g.has(1):
                        qg = g.mod(2, 1)
                        pe.wait_ge(xt_in[qg], adj_count(g, qg, 1))
                        if not dense and g.has(2):
                            w(pe, "edges16", g.at(2) + 1)
                        after(pe, "rfhi_ready", g, 0, g0)
                        pe.matmul(p_rf, xt_w[:, qg, :], wat[:, :], start=True, stop=True).then_inc(s["rf_ready"], 1)
                    if u.has(-1):
                        ql = u.mod(2, -1)
                        gl = g if k_in > 0 else Steps(g.pair, g.inner - 1, 2, ng)
                        y = yp[:, 0:P]
                        kl = (k_in - 1) % per_graph
                        if kl == 0:
                            w(pe, "rfb_ready", gl.at() + g0 + 1)
                            w(pe, "adjtsq_ready", gl.at() + g0 + 1)
                            after(pe, "yt_ready", gl, -1, g0)
                            pe.matmul(y, rfb[:, gl.mod(2), :], adjt_sq[:, gl.mod(2), :], start=True, stop=False)
                        w(pe, "msg_ready", u.at(-1) + u0 + 1)
                        final = kl == per_graph - 1
                        if final and not dense:
                            w(pe, "over_t_ready", gl.at() + 1)
                        rows = over_t[:, gl.mod(2), :] if (final and not dense) else ident[:, :]
                        pe.matmul(y, msg[:, ql, (R - 1) * P:UNIT], rows, start=False, stop=False)
                        w(pe, "sum3_ready", u.at(-1) + u0 + 1)
                        pe.matmul(y, sum3[:, ql, :], ident[:, :], start=False, stop=final).then_inc(s["summed"], 1)
                    if not dense and k_in == 0 and g.has(3):
                        w(pe, "cnt", g.at(3) + 1)
                        if g.has(1):
                            w(pe, "rfhi_ready", g.at(1) + 1)
                        pe.matmul(p_start, before[:, :], over_cnt[:, :], start=True, stop=True)\
                            .then_inc(s["start_ready"], 1)
                    if not dense and k_in == 1 and g.has(3):
                        w(pe, "slot_ready", g.at(3) + 1)
                        w(pe, "start_copied", g.at(3) + 1)
                        pe.matmul(p_over, slot_of[:, :], found[:, :], start=True, stop=True)\
                            .then_inc(s["over_gathered"], 1)
            schedule(pe, body)

        @block.vector
        def _(dve):
            def rank_edges(g):
                q, n = g.mod(2, 3), g.at(3) + 1
                dve.wait_ge(adj_in[q], g.pair * 16 + 16 * ((g.inner + 3) // 2 + 1))
                if not (g.static and not g.has(2)):
                    w(dve, "over_gathered", n - 1)
                    w(dve, "edges16", n - 1)
                alone(dve)
                adj = adj_w[:, q, :]
                dve.max(found[:, 0:8], adj).then_inc(s["top1"], 1)
                dve.tensor_reduce(least[:, bass.ds(g.at(3), 1)], adj, AX.X, ALU.min)
                w(dve, "top1", n)
                alone(dve)
                dve.match_replace(adj_r1[:, :], found[:, 0:8], adj, 0.0).then_inc(s["rest1"], 1)
                dve.max_index(found_idx[:, 0:8], found[:, 0:8], adj).then_inc(s["adj_read"], 1)
                w(dve, "rest1", n)
                alone(dve)
                dve.max(found[:, 8:16], adj_r1[:, :]).then_inc(s["top2"], 1)
                w(dve, "top2", n)
                alone(dve)
                dve.match_replace(adj_r2[:, :], found[:, 8:16], adj_r1[:, :], 0.0).then_inc(s["rest2"], 1)
                dve.max_index(found_idx[:, 8:16], found[:, 8:16], adj_r1[:, :])
                w(dve, "rest2", n)
                alone(dve)
                dve.max(found[:, 16:24], adj_r2[:, :]).then_inc(s["top3"], 1)
                w(dve, "top3", n)
                alone(dve)
                dve.tensor_scalar(over_bits[:, :], found[:, DIRECT:RANKS], 0.0, None, ALU.is_gt, ALU.add,
                                  accum_out=over_cnt[:, :]).then_inc(s["cnt"], 1)
                dve.max_index(found_idx[:, 16:24], found[:, 16:24], adj_r2[:, :]).then_inc(s["idx3"], 1)
                w(dve, "idx3", n)
                alone(dve)
                dve.tensor_copy(found[:, RANKS:2 * RANKS], found_idx[:, :]).then_inc(s["idxf"], 1)

            def place_overflow(g):
                n = g.at(3) + 1
                w(dve, "start_ready", n)
                w(dve, "idxf", n)
                start = found[:, 2 * RANKS:2 * RANKS + 1]
                dve.tensor_copy(start, p_start).then_inc(s["start_copied"], 1)
                w(dve, "start_copied", n)
                after(dve, "slot_ready", g, 2, 0)
                dve.tensor_scalar(slot_from[:, :], iota_row[:, :], start, None, ALU.is_ge)
                dve.tensor_tensor(over_end[:, bass.ds(g.at(3), 1)], start, over_cnt[:, :], ALU.add)\
                    .then_inc(s["from_ready"], 1)
                w(dve, "from_ready", n)
                dve.scalar_tensor_tensor(slot_of[:, :], iota_row[:, :], over_end[:, bass.ds(g.at(3), 1)],
                                         slot_from[:, :], ALU.is_lt, ALU.mult).then_inc(s["slot_ready"], 1)

            def finish_edges(g):
                q, n = g.mod(2, 2), g.at(2) + 1
                w(dve, "over_gathered", n)
                if not g.static or g.at(2) >= 2:
                    dve.wait_ge(edges_stored, 32 * (g.at(2) - 1))
                dve.tensor_scalar(rank_hit[:, :], iota_row[:, 0:OVER], p_over[:, 2 * RANKS:2 * RANKS + 1],
                                  iota_col[:, :], ALU.add, ALU.is_equal).then_inc(s["hits_ready"], 1)
                dve.tensor_copy(over_row[:, bass.ds(g.at(2), 1)], p_over[:, 2 * RANKS + 1:2 * RANKS + 2])
                dve.tensor_copy(last_rank[:, bass.ds(g.at(2), 1)], found[:, RANKS - 1:RANKS])
                dve.tensor_copy(ev[:, q, 0:DIRECT], found[:, 0:DIRECT])
                dve.tensor_copy(ei16[:, q, 0:DIRECT], found[:, RANKS:RANKS + DIRECT])
                w(dve, "hits_ready", n)
                dve.scalar_tensor_tensor(over_pick[:, 0, :], p_over[:, DIRECT:RANKS], 1.0, rank_hit[:, :],
                                         ALU.mult, ALU.mult, accum_out=ev[:, q, DIRECT:DIRECT + 1])
                dve.scalar_tensor_tensor(over_pick[:, 1, :], p_over[:, RANKS + DIRECT:2 * RANKS], 1.0,
                                         rank_hit[:, :], ALU.mult, ALU.mult,
                                         accum_out=ei[:, q, DIRECT:DIRECT + 1]).then_inc(s["picks_ready"], 1)
                w(dve, "picks_ready", n)
                dve.tensor_copy(ei16[:, q, DIRECT:DIRECT + 1], ei[:, q, DIRECT:DIRECT + 1]).then_inc(s["edges16"], 1)

            def body(pair):
                for i in range(per_pair):
                    u, g = unit(pair, i), graph(pair, i)
                    k_in = i % per_graph
                    if u.has(1):
                        q4 = u.mod(UNIT_BUFS, 1)
                        dve.wait_ge(unit_in[q4], unit_count(u, 1, q4))
                        after(dve, "rg_ready", u, -1, u0)
                        dve.tensor_scalar(pick[:, u.mod(2, 1), :], idx_bc[:, q4, :], iota_col[:, :], None,
                                          ALU.is_equal).then_inc(s["pick_ready"], 1)
                    if not dense and k_in == 0 and g.has(2):
                        finish_edges(g)
                    if not dense and k_in == 0 and g.has(0):
                        after_graph(dve, g, -2)
                        dve.tensor_scalar(over_t[:, g.mod(2), :], iota_row[:, :], over_row[:, bass.ds(g.at(), 1)], None,
                                          ALU.is_equal).then_inc(s["over_t_ready"], 1)
                    if not dense and k_in == 0 and g.has(3):
                        rank_edges(g)
                    if not dense and k_in == 1 and g.has(3):
                        place_overflow(g)
                    if k_in == 1 and g.has(-1):
                        w(dve, "u_ready", g.at(-1) + g0 + 1)
                        after(dve, "uh_ready", g, -2, g0)
                        dve.tensor_scalar(t_u[:, :], p_u, bd1c[:, :], None, ALU.add).then_inc(s["u_read"], 1)
                    if k_in == 1 and g.has(-2):
                        w(dve, "out_ready", g.at(-2) + g0 + 1)
                        w(dve, "xb_ready", g.at(-2) + g0 + 1)
                        dve.tensor_tensor(xres[:, g.at(-2), :], p_out, xb[:, g.mod(2), :], ALU.add)\
                            .then_inc(s["res_ready"], 1)
                    if u.has(0):
                        q, q4 = u.mod(2), u.mod(UNIT_BUFS)
                        w(dve, "wf_ready", u.at() + u0 + 1)
                        w(dve, "rfe_ready", u.at() + u0 + 1)
                        w(dve, "valsq_ready", u.at() + u0 + 1)
                        after(dve, "summed", u, -2, u0)
                        for r in range(R):
                            last = dve.scalar_tensor_tensor(
                                msg[:, q, r * P:(r + 1) * P], column(wf, r), val_sq[:, q4, r:r + 1],
                                rfe[:, q, r * P:(r + 1) * P], ALU.mult, ALU.mult)
                        last.then_inc(s["msg_ready"], 1)
                    if k_in == 1 and g.has(-1):
                        w(dve, "u_read", g.at(-1) + g0 + 1)
                        after(dve, "uexp_ready", g, -2, g0)
                        dve.tensor_scalar(t_cl[:, :], t_u[:, :], CLAMP, None, ALU.min)\
                            .then_inc(s["uclamped_ready"], 1)
                    if k_in == 0 and g.has(-2):
                        w(dve, "ulog_ready", g.at(-2) + g0 + 1)
                        after(dve, "out_ready", g, -3, g0)
                        dve.tensor_tensor(t_h[:, :], t_u[:, :], t_lg[:, :], ALU.max).then_inc(s["uh_ready"], 1)
                    if u.has(1):
                        w(dve, "log_ready", u.at(1) + u0 + 1)
                        after(dve, "wf_ready", u, -1, u0)
                        dve.tensor_tensor(hid[:, u.mod(2, 1), :], relz[:, :], logd[:, :], ALU.add)\
                            .then_inc(s["hid_ready"], 1)
            schedule(dve, body)

    with ExitStack() as c1:
        run(c1.enter_context(nc.Block()), dense=False)

    with ExitStack() as c1:
        chk = [phase_semaphore(nc, c0, k, f"chk{i}") for i in range(6)]
        bad = c1.enter_context(nc.sbuf_tensor("bad", [P, 3, B], F32))
        badn = c1.enter_context(nc.sbuf_tensor("badn", [P, 1], F32))
        onec = c1.enter_context(nc.sbuf_tensor("onec", [P, 1], F32))
        block = c1.enter_context(nc.Block())

        @block.vector
        def _(dve):
            dve.memset(onec[:, :], 1.0)
            dve.tensor_scalar(bad[:, 0, :], over_end[:, :], float(P), None, ALU.is_gt)
            dve.tensor_scalar(bad[:, 1, :], last_rank[:, :], 0.0, None, ALU.is_gt)
            dve.tensor_scalar(bad[:, 2, :], least[:, :], 0.0, None, ALU.is_lt).then_inc(chk[0], 1)
            dve.wait_ge(chk[0], 1)
            dve.tensor_reduce(badn[:, :], bad[:, :, :], AX.XY, ALU.add).then_inc(chk[1], 1)
            dve.wait_ge(chk[2], 1)
            dve.tensor_copy(flag[:, :], p_flag)

        @block.tensor
        def _(pe):
            pe.wait_ge(chk[1], 1)
            pe.matmul(p_flag, onec[:, :], badn[:, :], start=True, stop=True).then_inc(chk[2], 1)

    class Guarded:

        def __init__(self, block):
            self.block = block

        def _under_flag(self, of):
            def wrap(program):
                def guarded(eng):
                    overflow = eng.value_load(flag[0:1, 0:1], min_val=0, max_val=3 * B * P)
                    with eng.If(overflow > 0):
                        program(eng)
                of(guarded)
            return wrap

        sync = property(lambda self: self._under_flag(self.block.sync))
        gpsimd = property(lambda self: self._under_flag(self.block.gpsimd))
        scalar = property(lambda self: self._under_flag(self.block.scalar))
        tensor = property(lambda self: self._under_flag(self.block.tensor))
        vector = property(lambda self: self._under_flag(self.block.vector))

    with ExitStack() as c1:
        run(Guarded(c1.enter_context(nc.Block())), dense=True)


def layers12(nc, a, k):
    ctx = k["ctx"]
    xres, ident, deg, held = k["xres"], k["ident"], k["deg"], k["held"]
    dyn, agg = k["dyn"], k["agg"]
    NEG = -3.0e38

    with ExitStack() as c0:
        def sb(name, shape, dt=F32):
            return c0.enter_context(nc.sbuf_tensor("m_" + name, shape, dt))

        def ps(name):
            return c0.enter_context(nc.psum_tensor("m_" + name, [P, G, P], F32))

        wq_t, wk_t, wv = sb("wq_t", [P, P]), sb("wk_t", [P, P]), sb("wv", [P, P])
        w_layer, w_layer_t = sb("w_layer", [P, P]), sb("w_layer_t", [P, P])
        w_self, w_neigh = sb("w_self", [P, 1]), sb("w_neigh", [P, 1])
        conv_w = sb("conv_w", [P, 3, P])
        rows = sb("rows", [1, 4, P])
        mask = sb("mask", [P, B])
        wqk = sb("wqk", [P, P])
        att_self = sb("att_self", [P, 1])
        att_neigh = sb("att_neigh", [P, P])
        ones = sb("ones", [P, P])
        gamma4, beta4, bl4 = sb("gamma4", [P, G, P]), sb("beta4", [P, G, P]), sb("bl4", [P, G, P])
        conv_b4 = sb("conv_b4", [P, G, P])
        minus_half, dsafe, dpos, dpow = (sb(n, [P, G]) for n in ("minus_half", "dsafe", "dpos", "dpow"))

        adj_g, adjt_g = sb("adj_g", [P, 2, G, P]), sb("adjt_g", [P, 2, G, P])
        stats = {n: sb("stats_" + n, [P, G, 6]) for n in ("n0", "no", "n1", "n2")}
        mv = {n: sb("mv_" + n, [P, G, 2]) for n in stats}
        veps = {n: sb("veps_" + n, [P, G]) for n in stats}
        rstd = {n: sb("rstd_" + n, [P, G]) for n in stats}
        scratch = iter(range(B // G))

        def work():
            i = next(scratch)
            return k["xin"][:, i * G:(i + 1) * G, :]

        x1, x1b, x1t, qt, val = (sb(n, [P, G, P]) for n in ("x1", "x1b", "x1t", "qt", "val"))
        score = sb("score", [P, G, P])
        rest, esc, prob, prob_t = (work() for _ in range(4))
        top = sb("top", [P, G, 8])
        negmax, psum, rsum = sb("negmax", [P, G]), sb("psum", [P, G]), sb("rsum", [P, G])
        o1, o1n, o1g, r1 = (work() for _ in range(4))
        x2 = sb("x2", [P, 2, G, P])
        nb = sb("nb", [P, 2, G, P])
        x2t, hl, e2t = (sb(n, [P, G, P]) for n in ("x2t", "hl", "e2t"))
        lsum, leaky, logit, e2 = (work() for _ in range(4))
        a_self = sb("a_self", [P, G])
        negmax2, psum2, rsum2, rmask = (sb(n, [P, G]) for n in ("negmax2", "psum2", "rsum2", "rmask"))
        bm, xb2, o2, r2 = (work() for _ in range(4))
        xpad, xs, adj_i = sb("xpad", [P, G, P + 2]), sb("xs", [P, G, P]), sb("adj_i", [P, G, P])
        dinv = k["dinv"]

        pa, pb, pc = ps("pa"), ps("pb"), ps("pc")
        pd, pe_h, pf = ps("pd"), ps("pe_h"), ps("pf")
        pg, ph = ps("pg"), ps("ph")

        names = (
            "n0_mv n0_veps n0_rstd x1 x1b x1t_p x1t qt_p qt val_p val s_p score top negmax rest esc prob rsum "
            "probt_p probt o1_p o1 no_mv no_veps no_rstd o1n o1g r1 n1_mv n1_veps n1_rstd x2 "
            "nb deg x2t_p x2t as_p a_self h_p hl an_p lsum leaky logit negmax2 e2 rsum2 rmask e2t_p e2t o2_p o2 "
            "bm xb2 r2 n2_mv n2_veps n2_rstd x3 "
            "dsafe dpos dpow dinv xpad xs adj_i conv_p dyn agg_p agg n0_st no_st n1_st n2_st"
        ).split()
        s = {n: phase_semaphore(nc, c0, k, "m_" + n) for n in names}
        w_in = phase_semaphore(nc, c0, k, "m_w_in")
        adj_in = [phase_semaphore(nc, c0, k, f"m_adj_in{i}") for i in range(2)]
        adjt_in = [phase_semaphore(nc, c0, k, f"m_adjt_in{i}") for i in range(2)]
        pre = [phase_semaphore(nc, c0, k, f"m_pre{i}") for i in range(4)]

        with ExitStack() as c1:
            block = c1.enter_context(nc.Block())

            @block.sync
            def _(sp):
                for dst, src in ((wq_t, "wqt"), (wk_t, "wkt"), (wv, "wv"), (w_layer, "w_layer"),
                                 (w_layer_t, "w_layer_t"), (w_self, "w_self"), (w_neigh, "w_neigh"),
                                 (mask, "mask_rows")):
                    sp.dma_start(dst[:, :], a[src]).then_inc(w_in, 16)
                sp.dma_start(conv_w[:, :, :], a["conv_wt"]).then_inc(w_in, 16)
                for j, src in enumerate(("gamma_row", "beta_row", "b_layer_row", "conv_b_row")):
                    sp.dma_start(rows[:, j, :], a[src]).then_inc(w_in, 16)

            @block.vector
            def _(dve):
                dve.memset(minus_half[:, :], -0.5)
                dve.memset(xpad[:, :, :], 0.0)
                dve.memset(ones[:, :], 1.0).then_inc(pre[0], 1)
                dve.wait_ge(pre[1], 1)
                dve.tensor_scalar(wqk[:, :], pa[:, 0, :], float(P) ** -0.5, None, ALU.mult)
                dve.tensor_copy(att_self[:, :], pa[:, 1, 0:1])
                dve.wait_ge(pre[0], 1)
                dve.tensor_scalar(att_neigh[:, :], ones[:, :], pa[:, 2, 0:1], None, ALU.mult)
                for j, dst in enumerate((gamma4, beta4, bl4, conv_b4)):
                    dve.tensor_copy(dst[:, :, :], pb[:, j:j + 1, :].broadcast_to((P, G, P)))

            @block.tensor
            def _(pe):
                pe.wait_ge(w_in, 16 * 13)
                pe.wait_ge(pre[0], 1)
                pe.matmul(pa[:, 0, :], wq_t[:, :], wk_t[:, :], start=True, stop=True)
                pe.matmul(pa[:, 1, 0:1], w_layer_t[:, :], w_self[:, :], start=True, stop=True)
                pe.matmul(pa[:, 2, 0:1], w_layer_t[:, :], w_neigh[:, :], start=True, stop=True)
                for j in range(4):
                    last = pe.matmul(pb[:, j, :], ones[0:1, :], rows[:, j, :], start=True, stop=True)
                last.then_inc(pre[1], 1)

        NGR = B // G

        def schedule(eng, body):
            pairs(eng, (0, 1), (2, NGR // 2 - 1), (NGR // 2 - 1, NGR // 2, NGR // 2 + 1), body)

        def steps(pair):
            for i in range(2):
                g = Steps(pair, i, 2, NGR)
                yield g, g.has(0), g.has(-1), g.has(-2), g.has(-3)

        def w(eng, name, g, d=0):
            eng.wait_ge(s[name], g.at(d) + 1)

        def after(eng, name, g, d):
            if not g.static or g.at(d) >= 0:
                eng.wait_ge(s[name], min(g.at(d), NGR - 1) + 1 if g.static else g.at(d) + 1)

        def landed(eng, sems, g, d=0):
            eng.wait_ge(sems[g.mod(2, d)], g.pair * 16 + 16 * ((g.inner + d) // 2 + 1))

        with ExitStack() as c1:
            block = c1.enter_context(nc.Block())

            def four(g, d=0):
                return bass.ds(g.at(d) * G, G)

            @block.sync
            def _(sp):
                def load(g, d):
                    q = g.mod(2, d)
                    sp.dma_start(adj_g[:, q, :, :], a["adj_rows"][:, four(g, d), :]).then_inc(adj_in[q], 16)

                def load_t(g, d):
                    q = g.mod(2, d)
                    sp.dma_start(adjt_g[:, q, :, :], a["adj_t"][:, four(g, d), :]).then_inc(adjt_in[q], 16)

                def body(pair):
                    for g, one, tail, two, three in steps(pair):
                        if g.static and g.at() == 0:
                            load(g, 0)
                        if g.has(1):
                            after(sp, "score", g, -1)
                            after(sp, "deg", g, -1)
                            after(sp, "nb", g, -1)
                            sp.sem_inc(held["SP"], 1)
                            load(g, 1)
                        if g.has(-2):
                            after(sp, "adj_i", g, -4)
                            sp.sem_inc(held["SP"], 1)
                            load_t(g, -2)
                schedule(sp, body)

            @block.gpsimd
            def _(pool):
                def rstd_of(g, d, n):
                    w(pool, n + "_mv", g, d)
                    pool.sem_inc(held["Pool"], 1)
                    pool.tensor_scalar(veps[n][:, :], mv[n][:, :, 1], EPS, None, ALU.add).then_inc(s[n + "_veps"], 1)
                    w(pool, n + "_veps", g, d)
                    pool.tensor_tensor(rstd[n][:, :], veps[n][:, :], minus_half[:, :], ALU.pow)\
                        .then_inc(s[n + "_rstd"], 1)

                def body(pair):
                    for g, one, tail, two, three in steps(pair):
                        if one:
                            rstd_of(g, 0, "n0")
                        if tail:
                            w(pool, "o1n", g, -1)
                            after(pool, "r1", g, -2)
                            pool.tensor_tensor(o1g[:, :, :], o1n[:, :, :], gamma4[:, :, :], ALU.mult)\
                                .then_inc(s["o1g"], 1)
                            w(pool, "o1g", g, -1)
                            w(pool, "x1b", g, -1)
                            after(pool, "x2", g, -2)
                            pool.tensor_tensor(r1[:, :, :], o1g[:, :, :], x1b[:, :, :], ALU.add).then_inc(s["r1"], 1)
                        if one:
                            w(pool, "x1", g)
                            after(pool, "r1", g, -1)
                            pool.tensor_tensor(x1b[:, :, :], x1[:, :, :], beta4[:, :, :], ALU.add)\
                                .then_inc(s["x1b"], 1)
                        if three:
                            w(pool, "x3", g, -3)
                            after(pool, "conv_p", g, -4)
                            pool.sem_inc(held["Pool"], 1)
                            pool.tensor_copy(xpad[:, :, 1:P + 1], xres[:, four(g, -3), :]).then_inc(s["xpad"], 1)
                            landed(pool, adjt_in, g, -3)
                            after(pool, "agg_p", g, -4)
                            pool.tensor_tensor(adj_i[:, :, :], adjt_g[:, g.mod(2, -3), :, :],
                                               ident[:, :].unsqueeze(1).broadcast_to((P, G, P)), ALU.add)\
                                .then_inc(s["adj_i"], 1)
                        if tail:
                            landed(pool, adj_in, g, -1)
                            after(pool, "logit", g, -3)
                            pool.sem_inc(held["Pool"], 1)
                            pool.tensor_scalar(nb[:, g.mod(2, -1), :, :], adj_g[:, g.mod(2, -1), :, :], -1.0, 1.0e10,
                                               ALU.add, ALU.mult).then_inc(s["nb"], 1)
                            rstd_of(g, -1, "n1")
                        if one:
                            w(pool, "deg", g)
                            after(pool, "dpow", g, -1)
                            pool.sem_inc(held["Pool"], 1)
                            pool.tensor_scalar(dsafe[:, :], deg[:, g.mod(2), :], 1.0, 1.2e-38, ALU.add, ALU.max)\
                                .then_inc(s["dsafe"], 1)
                            after(pool, "dinv", g, -1)
                            pool.sem_inc(held["Pool"], 1)
                            pool.tensor_scalar(dpos[:, :], deg[:, g.mod(2), :], 1.0, 0.0, ALU.add, ALU.is_gt)\
                                .then_inc(s["dpos"], 1)
                            w(pool, "dsafe", g)
                            pool.tensor_tensor(dpow[:, :], dsafe[:, :], minus_half[:, :], ALU.pow)\
                                .then_inc(s["dpow"], 1)
                            w(pool, "dpow", g)
                            w(pool, "dpos", g)
                            pool.sem_inc(held["Pool"], 1)
                            pool.tensor_tensor(dinv[:, four(g)], dpow[:, :], dpos[:, :], ALU.mult)\
                                .then_inc(s["dinv"], 1)
                        if two:
                            after(pool, "xb2", g, -3)
                            pool.sem_inc(held["Pool"], 1)
                            pool.tensor_tensor(bm[:, :, :], bl4[:, :, :],
                                               mask[:, four(g, -2)].unsqueeze(2).broadcast_to((P, G, P)), ALU.mult)\
                                .then_inc(s["bm"], 1)
                            w(pool, "bm", g, -2)
                            w(pool, "x2", g, -2)
                            after(pool, "r2", g, -3)
                            pool.tensor_tensor(xb2[:, :, :], bm[:, :, :], x2[:, g.mod(2, -2), :, :], ALU.add)\
                                .then_inc(s["xb2"], 1)
                            rstd_of(g, -2, "n2")
                        if one:
                            rstd_of(g, 0, "no")
                schedule(pool, body)

            @block.scalar
            def _(act):
                act.preload_act_table_set("natural_log_exp_and_others")

                def evac(g, d, dst, src, ready, done):
                    w(act, ready, g, d)
                    return act.activation(dst, src, ACT.Copy).then_inc(s[done], 1)

                def body(pair):
                    for g, one, tail, two, three in steps(pair):
                        if two:
                            after(act, "an_p", g, -3)
                            evac(g, -2, x2t[:, :, :], pd[:, :, :], "x2t_p", "x2t")
                            after(act, "o2_p", g, -3)
                            evac(g, -2, hl[:, :, :], pe_h[:, :, :], "h_p", "hl")
                        if one:
                            after(act, "s_p", g, -1)
                            evac(g, 0, x1t[:, :, :], pa[:, :, :], "x1t_p", "x1t")
                            evac(g, 0, qt[:, :, :], pb[:, :, :], "qt_p", "qt")
                            after(act, "o1_p", g, -1)
                            evac(g, 0, val[:, :, :], pc[:, :, :], "val_p", "val")
                        if two:
                            w(act, "negmax2", g, -2)
                            after(act, "e2t_p", g, -3)
                            after(act, "rsum2", g, -3)
                            for j in range(G):
                                last = act.activation(e2[:, j, :], logit[:, j, :], ACT.Exp, bias=negmax2[:, j:j + 1],
                                                      accum_out=psum2[:, j:j + 1])
                            last.then_inc(s["e2"], 1)
                        if one:
                            w(act, "negmax", g)
                            after(act, "prob", g, -1)
                            for j in range(G):
                                last = act.activation(esc[:, j, :], score[:, j, :], ACT.Exp, bias=negmax[:, j:j + 1])
                            last.then_inc(s["esc"], 1)
                        if two:
                            evac(g, -2, e2t[:, :, :], pd[:, :, :], "e2t_p", "e2t")
                        if three:
                            evac(g, -3, agg[:, four(g, -3), :], ph[:, :, :], "agg_p", "agg")
                        if one:
                            evac(g, 0, prob_t[:, :, :], pb[:, :, :], "probt_p", "probt")
                schedule(act, body)

            @block.tensor
            def _(pe):
                def body(pair):
                    for g, one, tail, two, three in steps(pair):
                        if two:
                            w(pe, "x2", g, -2)
                            after(pe, "e2t", g, -3)
                            for j in range(G):
                                last = pe.transpose(pd[:, j, :], x2[:, g.mod(2, -2), j, :], ident[:, :])
                            last.then_inc(s["x2t_p"], 1)
                            w(pe, "x2t", g, -2)
                            for j in range(G):
                                last = pe.matmul(pd[:, 0, j:j + 1], x2t[:, j, :], att_self[:, :], start=True, stop=True)
                            last.then_inc(s["as_p"], 1)
                            for j in range(G):
                                last = pe.matmul(pe_h[:, j, :], x2t[:, j, :], w_layer[:, :], start=True, stop=True)
                            last.then_inc(s["h_p"], 1)
                            after(pe, "o2", g, -3)
                            pe.matmul(pf[:, :, :], att_neigh[:, :], x2t[:, :, :], start=True, stop=True)\
                                .then_inc(s["an_p"], 1)
                        if one:
                            w(pe, "x1", g)
                            after(pe, "o1", g, -1)
                            for j in range(G):
                                last = pe.transpose(pa[:, j, :], x1[:, j, :], ident[:, :])
                            last.then_inc(s["x1t_p"], 1)
                            w(pe, "x1t", g)
                            pe.matmul(pb[:, :, :], wqk[:, :], x1t[:, :, :], start=True, stop=True)\
                                .then_inc(s["qt_p"], 1)
                            after(pe, "val", g, -1)
                            for j in range(G):
                                last = pe.matmul(pc[:, j, :], x1t[:, j, :], wv[:, :], start=True, stop=True)
                            last.then_inc(s["val_p"], 1)
                            w(pe, "qt", g)
                            for j in range(G):
                                last = pe.matmul(pa[:, j, :], qt[:, j, :], x1t[:, j, :], start=True, stop=True)
                            last.then_inc(s["s_p"], 1)
                        if three:
                            w(pe, "xpad", g, -3)
                            after(pe, "dyn", g, -4)
                            for j in range(G):
                                for kk in range(3):
                                    last = pe.matmul(pg[:, j, :], xpad[:, j, kk:kk + P], conv_w[:, kk, :],
                                                     start=kk == 0, stop=kk == 2)
                            last.then_inc(s["conv_p"], 1)
                            w(pe, "xs", g, -3)
                            w(pe, "adj_i", g, -3)
                            after(pe, "agg", g, -4)
                            for j in range(G):
                                last = pe.matmul(ph[:, j, :], xs[:, j, :], adj_i[:, j, :], start=True, stop=True)
                            last.then_inc(s["agg_p"], 1)
                        if two:
                            w(pe, "e2", g, -2)
                            w(pe, "a_self", g, -2)
                            for j in range(G):
                                last = pe.transpose(pd[:, j, :], e2[:, j, :], ident[:, :])
                            last.then_inc(s["e2t_p"], 1)
                            w(pe, "e2t", g, -2)
                            w(pe, "hl", g, -2)
                            w(pe, "lsum", g, -2)
                            for j in range(G):
                                last = pe.matmul(pf[:, j, :], e2t[:, j, :], hl[:, j, :], start=True, stop=True)
                            last.then_inc(s["o2_p"], 1)
                        if one:
                            w(pe, "prob", g)
                            for j in range(G):
                                last = pe.transpose(pb[:, j, :], prob[:, j, :], ident[:, :])
                            last.then_inc(s["probt_p"], 1)
                            w(pe, "probt", g)
                            w(pe, "val", g)
                            w(pe, "score", g)
                            for j in range(G):
                                last = pe.matmul(pa[:, j, :], prob_t[:, j, :], val[:, j, :], start=True, stop=True)
                            last.then_inc(s["o1_p"], 1)
                schedule(pe, body)

            @block.vector
            def _(dve):
                def moments(g, d, n, x):
                    after(dve, n + "_mv", g, d - 1)
                    for j in range(G):
                        last = dve.bn_stats(stats[n][:, j, :], x(j))
                    last.then_inc(s[n + "_st"], 1)
                    w(dve, n + "_st", g, d)
                    after(dve, n + "_rstd", g, d - 1)
                    after(dve, {"n0": "x1", "no": "o1n", "n1": "x2", "n2": "x3"}[n], g, d - 1)
                    dve.sem_inc(held["DVE"], 1)
                    for j in range(G):
                        last = dve.bn_aggr(mv[n][:, j, :], stats[n][:, j, :])
                    last.then_inc(s[n + "_mv"], 1)

                def normalise(g, d, n, dst, x, done):
                    w(dve, n + "_rstd", g, d)
                    for j in range(G):
                        last = dve.tensor_scalar(dst(j), x(j), mv[n][:, j, 0:1], rstd[n][:, j:j + 1],
                                                 ALU.subtract, ALU.mult)
                    last.then_inc(s[done], 1)

                def bc(t):
                    return t.unsqueeze(2).broadcast_to((P, G, P))

                def one_graph(g, d, j):
                    return bass.ds(g.at(d) * G + j, 1)

                def body(pair):
                    for g, one, tail, two, three in steps(pair):
                        if three:
                            after(dve, "agg_p", g, -4)
                            w(dve, "x3", g, -3)
                            w(dve, "dinv", g, -3)
                            dve.tensor_tensor(xs[:, :, :], xres[:, four(g, -3), :], bc(dinv[:, four(g, -3)]), ALU.mult)\
                                .then_inc(s["xs"], 1)
                        if one:
                            x0 = lambda j: xres[:, one_graph(g, 0, j), :].rearrange("p a n -> p (a n)")
                            moments(g, 0, "n0", x0)
                        if tail:
                            after(dve, "o1g", g, -2)
                            normalise(g, -1, "no", lambda j: o1n[:, j, :], lambda j: o1[:, j, :], "o1n")
                        if two:
                            w(dve, "as_p", g, -2)
                            after(dve, "lsum", g, -3)
                            dve.tensor_copy(a_self[:, :], pd[:, 0, 0:G]).then_inc(s["a_self"], 1)
                        if one:
                            after(dve, "x1t_p", g, -1)
                            after(dve, "x1b", g, -1)
                            normalise(g, 0, "n0", lambda j: x1[:, j, :], x0, "x1")
                        if two:
                            w(dve, "an_p", g, -2)
                            w(dve, "a_self", g, -2)
                            after(dve, "leaky", g, -3)
                            dve.tensor_tensor(lsum[:, :, :], pf[:, :, :], bc(a_self[:, :]), ALU.add)\
                                .then_inc(s["lsum"], 1)
                            w(dve, "lsum", g, -2)
                            after(dve, "logit", g, -3)
                            dve.scalar_tensor_tensor(leaky[:, :, :], lsum[:, :, :], 0.2, lsum[:, :, :], ALU.mult,
                                                     ALU.max).then_inc(s["leaky"], 1)
                            w(dve, "leaky", g, -2)
                            w(dve, "nb", g, -2)
                            after(dve, "e2", g, -3)
                            dve.tensor_tensor(logit[:, :, :], leaky[:, :, :], nb[:, g.mod(2, -2), :, :], ALU.add)\
                                .then_inc(s["logit"], 1)
                            w(dve, "logit", g, -2)
                            dve.tensor_reduce(negmax2[:, :], logit[:, :, :], AX.X, ALU.max, negate=True)\
                                .then_inc(s["negmax2"], 1)
                        if tail:
                            w(dve, "r1", g, -1)
                            moments(g, -1, "n1", lambda j: r1[:, j, :])
                        if one:
                            landed(dve, adj_in, g)
                            after(dve, "dinv", g, -2)
                            dve.tensor_reduce(deg[:, g.mod(2), :], adj_g[:, g.mod(2), :, :], AX.X, ALU.add)\
                                .then_inc(s["deg"], 1)
                            w(dve, "s_p", g)
                            after(dve, "esc", g, -1)
                            after(dve, "rest", g, -1)
                            dve.tensor_tensor(score[:, :, :], pa[:, :, :], adj_g[:, g.mod(2), :, :], ALU.add)\
                                .then_inc(s["score"], 1)
                            after(dve, "rest", g, -1)
                            w(dve, "score", g)
                            dve.sem_inc(held["DVE"], 1)
                            for j in range(G):
                                last = dve.max(top[:, j, :], score[:, j, :])
                            last.then_inc(s["top"], 1)
                            w(dve, "top", g)
                            dve.tensor_scalar(negmax[:, :], top[:, :, 0], -1.0, None, ALU.mult)\
                                .then_inc(s["negmax"], 1)
                            after(dve, "prob", g, -1)
                            dve.sem_inc(held["DVE"], 1)
                            for j in range(G):
                                last = dve.match_replace(rest[:, j, :], top[:, j, :], score[:, j, :], NEG)
                            last.then_inc(s["rest"], 1)
                        if three:
                            w(dve, "conv_p", g, -3)
                            dve.tensor_tensor(dyn[:, :, four(g, -3)].rearrange("p t b -> p b t"), pg[:, :, :],
                                              conv_b4[:, :, :], ALU.add).then_inc(s["dyn"], 1)
                        if tail:
                            after(dve, "x2t_p", g, -3)
                            after(dve, "xb2", g, -3)
                            normalise(g, -1, "n1", lambda j: x2[:, g.mod(2, -1), j, :], lambda j: r1[:, j, :], "x2")
                        if two:
                            w(dve, "e2", g, -2)
                            dve.reciprocal(rsum2[:, :], psum2[:, :]).then_inc(s["rsum2"], 1)
                            w(dve, "rsum2", g, -2)
                            after(dve, "o2", g, -3)
                            dve.tensor_tensor(rmask[:, :], rsum2[:, :], mask[:, four(g, -2)], ALU.mult)\
                                .then_inc(s["rmask"], 1)
                        if one:
                            w(dve, "esc", g)
                            w(dve, "rest", g)
                            after(dve, "probt_p", g, -1)
                            after(dve, "rsum", g, -1)
                            for j in range(G):
                                last = dve.scalar_tensor_tensor(prob[:, j, :], rest[:, j, :], -1.0e38, esc[:, j, :],
                                                                ALU.is_lt, ALU.mult, accum_out=psum[:, j:j + 1])
                            last.then_inc(s["prob"], 1)
                            w(dve, "prob", g)
                            after(dve, "o1", g, -1)
                            dve.reciprocal(rsum[:, :], psum[:, :]).then_inc(s["rsum"], 1)
                        if two:
                            w(dve, "o2_p", g, -2)
                            w(dve, "rmask", g, -2)
                            after(dve, "r2", g, -3)
                            dve.tensor_tensor(o2[:, :, :], pf[:, :, :], bc(rmask[:, :]), ALU.mult).then_inc(s["o2"], 1)
                            w(dve, "o2", g, -2)
                            w(dve, "xb2", g, -2)
                            after(dve, "x3", g, -3)
                            dve.tensor_tensor(r2[:, :, :], o2[:, :, :], xb2[:, :, :], ALU.add).then_inc(s["r2"], 1)
                            w(dve, "r2", g, -2)
                            moments(g, -2, "n2", lambda j: r2[:, j, :])
                        if one:
                            w(dve, "o1_p", g)
                            w(dve, "rsum", g)
                            after(dve, "o1n", g, -1)
                            dve.tensor_tensor(o1[:, :, :], pa[:, :, :], bc(rsum[:, :]), ALU.mult).then_inc(s["o1"], 1)
                            w(dve, "o1", g)
                            moments(g, 0, "no", lambda j: o1[:, j, :])
                        if two:
                            normalise(g, -2, "n2", lambda j: xres[:, one_graph(g, -2, j), :]
                                      .rearrange("p a n -> p (a n)"), lambda j: r2[:, j, :], "x3")
                schedule(dve, body)

        clear_semaphores(nc, k)


def lstm(nc, a, k):
    dyn, agg, xres, ident, dinv, out, held = (k[n] for n in ("dyn", "agg", "xres", "ident", "dinv", "out", "held"))
    hs = k["xin"][:, :, :].rearrange("p g n -> p (g n)").rearrange("p (t b) -> p t b", b=B)
    with ExitStack() as c0:
        def sb(name, shape, dt=F32):
            return c0.enter_context(nc.sbuf_tensor("r_" + name, shape, dt))

        def sem(name):
            return phase_semaphore(nc, c0, k, "r_" + name)

        w_ih, w_hh = sb("w_ih", [P, 4, P]), sb("w_hh", [P, 4, P])
        b_ih, b_hh, bias = (sb(n, [3, 4, P]) for n in ("b_ih", "b_hh", "bias"))
        left = [sb(f"left{i}", [3, 4, P]) for i in range(2)]
        rounded = [sb(f"rounded{i}", [3, 4, P], BF16) for i in range(3)]
        own_row = [sb(f"own_row{i}", [3, 1]) for i in range(3)]
        merged = [sb(f"merged{i}", [3, 4, P]) for i in range(2)]
        bias_parts = sb("bias_parts", [3, 4, P], BF16)
        ones = sb("ones", [3, 2 * B], BF16)
        h0 = sb("h0", [P, B])
        gates = sb("gates", [P, 4, B])
        cell = sb("cell", [P, B])
        keep, new, tanh_c = sb("keep", [P, B]), sb("new", [P, B]), sb("tanh_c", [P, B])
        weights_in, prep_a, prep_b = sem("weights_in"), sem("prep_a"), sem("prep_b")
        x_part, z_ready, zo_ready, gates_ready, keep_ready, new_ready, cell_ready, tanh_ready, h_ready = (
            sem(n) for n in ("x_part", "z_ready", "zo_ready", "gates_ready", "keep_ready", "new_ready", "cell_ready",
                             "tanh_ready", "h_ready"))
        z_ifg = [c0.enter_context(nc.psum_tensor(f"r_z{i}", [P, 3, 2 * B], F32)) for i in range(2)]
        z_o = [c0.enter_context(nc.psum_tensor(f"r_zo{i}", [P, 4, 2 * B], F32)) for i in range(2)]
        I_, F_, G_, O_ = range(4)

        def z_of(bank, q):
            return z_o[bank][:, 0, :] if q == O_ else z_ifg[bank][:, q, :]

        with ExitStack() as c1:
            block = c1.enter_context(nc.Block())

            @block.sync
            def _(sp):
                for dst, src in ((w_ih, "w_iht"), (w_hh, "w_hht")):
                    sp.dma_start(dst[:, :, :].rearrange("p a n -> p (a n)"), a[src]).then_inc(weights_in, 16)
                for dst, src in ((b_ih, "b_ih_row"), (b_hh, "b_hh_row")):
                    sp.dma_start(dst[:, :, :].rearrange("p a n -> p (a n)"), a[src].broadcast_to((3, 4 * P)))\
                        .then_inc(weights_in, 16)

            @block.vector
            def _(dve):
                dve.memset(h0[:, :], 0.0)
                dve.memset(cell[:, :], 0.0)
                dve.memset(ones[:, :], 1.0)
                dve.wait_ge(weights_in, 64)
                for q in (I_, F_, O_):
                    dve.tensor_scalar(w_ih[:, q, :], w_ih[:, q, :], 0.5, None, ALU.mult)
                for row in range(3):
                    dve.tensor_scalar(own_row[row][:, :], k["iota_col"][0:3, :], float(row), None, ALU.is_equal)
                dve.tensor_tensor(bias[:, :, :], b_ih[:, :, :], b_hh[:, :, :], ALU.add).then_inc(prep_a, 1)
                dve.wait_ge(prep_a, 1)
                for q in (I_, F_, O_):
                    last = dve.tensor_scalar(bias[:, q, :], bias[:, q, :], 0.5, None, ALU.mult)
                last.then_inc(prep_a, 1)
                dve.wait_ge(prep_a, 2)
                dve.tensor_copy(rounded[0][:, :, :], bias[:, :, :]).then_inc(prep_a, 1)
                dve.wait_ge(prep_a, 3)
                dve.tensor_tensor(left[0][:, :, :], bias[:, :, :], rounded[0][:, :, :], ALU.subtract)\
                    .then_inc(prep_a, 1)
                dve.wait_ge(prep_a, 4)
                dve.tensor_copy(rounded[1][:, :, :], left[0][:, :, :]).then_inc(prep_a, 1)
                dve.wait_ge(prep_a, 5)
                dve.tensor_tensor(left[1][:, :, :], left[0][:, :, :], rounded[1][:, :, :], ALU.subtract)\
                    .then_inc(prep_a, 1)
                dve.wait_ge(prep_a, 6)
                dve.tensor_scalar(merged[0][:, :, :], rounded[0][:, :, :], own_row[0][:, :], None, ALU.mult)\
                    .then_inc(prep_a, 1)
                dve.wait_ge(prep_a, 7)
                dve.scalar_tensor_tensor(merged[1][:, :, :], rounded[1][:, :, :], own_row[1][:, :],
                                         merged[0][:, :, :], ALU.mult, ALU.add).then_inc(prep_a, 1)
                dve.wait_ge(prep_a, 8)
                dve.scalar_tensor_tensor(bias_parts[:, :, :], left[1][:, :, :], own_row[2][:, :],
                                         merged[1][:, :, :], ALU.mult, ALU.add)
                for q in range(4):
                    dve.tensor_scalar(w_hh[:, q, :], w_hh[:, q, :], 0.5 if q == G_ else 0.25, None, ALU.mult)

        with ExitStack() as c1:
            block = c1.enter_context(nc.Block())

            def quads(eng, body):
                body(0, True, False)
                with eng.Fori(1, P // 4 - 1) as quad:
                    body(quad * 4, False, False)
                body(P - 4, False, True)

            @block.tensor
            def _(pe):
                def inputs(t, bank, gates_of):
                    for q in gates_of:
                        z = z_of(bank, q)
                        pe.matmul(z, bias_parts[:, q, :], ones[:, :], start=q in (G_, O_), stop=False,
                                  skip_group_check=True)
                        pe.matmul(z, w_ih[:, q, :], dyn[:, bass.ds(t, 2), :], start=False, stop=False,
                                  skip_group_check=True)

                def recurrence(t, j, h):
                    for q in (G_, I_, F_, O_):
                        last = pe.matmul(z_of(j // 2, q)[:, (j % 2) * B:(j % 2 + 1) * B], w_hh[:, q, :], h,
                                         start=False, stop=True, skip_group_check=True)
                        if q == F_:
                            last.then_inc(z_ready, 1)
                    last.then_inc(zo_ready, 1)

                def body(t, first, final):
                    if first:
                        inputs(0, 0, (G_, I_, F_, O_))
                    for j in range(4):
                        if first and j == 0:
                            h = h0[:, :]
                        else:
                            pe.wait_ge(h_ready, t + j)
                            h = hs[:, bass.ds(t + (j - 1), 1), :]
                        recurrence(t, j, h)
                        part = (G_, I_) if j % 2 == 0 else (F_, O_)
                        if j < 2:
                            inputs(t + 2, 1, part)
                        elif not final:
                            inputs(t + 4, 0, part)
                quads(pe, body)

            @block.scalar
            def _(act):
                def body(t, first, final):
                    for j in range(4):
                        act.wait_ge(z_ready, t + (j + 1))
                        if not (first and j == 0):
                            act.wait_ge(h_ready, t + j)
                        step = slice((j % 2) * B, (j % 2 + 1) * B)
                        act.activation(gates[:, 0:3, :], z_ifg[j // 2][:, :, step], ACT.Tanh).then_inc(gates_ready, 1)
                        act.wait_ge(zo_ready, t + (j + 1))
                        act.activation(gates[:, O_, :], z_o[j // 2][:, 0, step], ACT.Tanh)
                        act.wait_ge(cell_ready, t + (j + 1))
                        act.activation(tanh_c[:, :], cell[:, :], ACT.Tanh, scale=0.5).then_inc(tanh_ready, 1)
                quads(act, body)

            @block.vector
            def _(dve):
                def body(t, first, final):
                    for j in range(4):
                        n = t + (j + 1)
                        dve.wait_ge(gates_ready, n)
                        dve.scalar_tensor_tensor(keep[:, :], gates[:, F_, :], 1.0, cell[:, :], ALU.add, ALU.mult)
                        dve.scalar_tensor_tensor(new[:, :], gates[:, I_, :], 1.0, gates[:, G_, :], ALU.add, ALU.mult)\
                            .then_inc(new_ready, 1)
                        dve.wait_ge(new_ready, n)
                        dve.scalar_tensor_tensor(cell[:, :], keep[:, :], 0.5, new[:, :], ALU.mult, ALU.add)\
                            .then_inc(cell_ready, 1)
                        dve.wait_ge(tanh_ready, n)
                        dve.scalar_tensor_tensor(hs[:, bass.ds(t + j, 1), :].rearrange("p a b -> p (a b)"),
                                                 gates[:, O_, :], 1.0, tanh_c[:, :],
                                                 ALU.add, ALU.mult).then_inc(h_ready, 1)
                quads(dve, body)

        h4, agg4 = sb("h4", [P, 2, G, P]), sb("agg4", [P, 2, G, P])
        lw, act_out, r3, y = (sb(n, [P, 2, G, P]) for n in ("lw", "act_out", "r3", "y"))
        stats, mv = sb("stats", [P, G, 6]), sb("mv", [P, G, 2])
        veps, rstd, minus_half = sb("veps", [P, G]), sb("rstd", [P, G]), sb("minus_half", [P, G])
        hdinv = sb("hdinv", [P, B])
        names = ("h4_ready agg4_ready lwt_p lw_ready o_p act_ready r3_ready st_ready mv_ready veps_ready rstd_ready "
                 "y_ready consts").split()
        s = {n: sem(n) for n in names}
        stored = [sem(f"stored{i}") for i in range(2)]
        lwt_b = [z_o[i][:, :, :] for i in range(2)]
        o_b = [c0.enter_context(nc.psum_tensor(f"r_o{i}", [P, G, P], F32)) for i in range(2)]
        NGR = B // G

        def schedule(eng, body):
            pairs(eng, (0,), (1, NGR // 2), (NGR // 2,), body)

        def steps(pair):
            for i in range(2):
                g = Steps(pair, i, 2, NGR)
                yield g, g.has(0), g.has(-1)

        def w(eng, name, g, d=0):
            eng.wait_ge(s[name], g.at(d) + 1)

        def after(eng, name, g, d):
            if not g.static or g.at(d) >= 0:
                eng.wait_ge(s[name], min(g.at(d), NGR - 1) + 1 if g.static else g.at(d) + 1)

        with ExitStack() as c1:
            block = c1.enter_context(nc.Block())

            @block.sync
            def _(sp):
                def body(pair):
                    for g, one, two in steps(pair):
                        if two:
                            q = g.mod(2, -1)
                            w(sp, "y_ready", g, -1)
                            sp.sem_inc(held["SP"], 1)
                            sp.dma_start(out[bass.ds(g.at(-1) * G, G), :, :].rearrange("b i d -> i b d"),
                                         y[:, q, :, :]).then_inc(stored[q], 16)
                schedule(sp, body)
                for q in range(2):
                    sp.wait_ge(stored[q], 16 * (NGR // 2))

            @block.gpsimd
            def _(pool):
                pool.memset(minus_half[:, :], -0.5).then_inc(s["consts"], 1)
                pool.wait_ge(s["consts"], 1)

                def body(pair):
                    for g, one, two in steps(pair):
                        if one:
                            after(pool, "o_p", g, -2)
                            pool.sem_inc(held["Pool"], 1)
                            pool.tensor_copy(agg4[:, g.mod(2), :, :], agg[:, bass.ds(g.at() * G, G), :])\
                                .then_inc(s["agg4_ready"], 1)
                        if two:
                            w(pool, "mv_ready", g, -1)
                            pool.sem_inc(held["Pool"], 1)
                            pool.tensor_scalar(veps[:, :], mv[:, :, 1], EPS, None, ALU.add)\
                                .then_inc(s["veps_ready"], 1)
                            w(pool, "veps_ready", g, -1)
                            pool.tensor_tensor(rstd[:, :], veps[:, :], minus_half[:, :], ALU.pow)\
                                .then_inc(s["rstd_ready"], 1)
                schedule(pool, body)

            @block.tensor
            def _(pe):
                def body(pair):
                    for g, one, two in steps(pair):
                        q = g.mod(2)
                        if one:
                            w(pe, "h4_ready", g)
                            after(pe, "lw_ready", g, -2)
                            for j in range(G):
                                last = pe.transpose(lwt_b[q][:, j, :], h4[:, q, j, :], ident[:, :])
                            last.then_inc(s["lwt_p"], 1)
                        if two:
                            q = g.mod(2, -1)
                            w(pe, "lw_ready", g, -1)
                            w(pe, "agg4_ready", g, -1)
                            after(pe, "act_ready", g, -3)
                            for j in range(G):
                                last = pe.matmul(o_b[q][:, j, :], agg4[:, q, j, :], lw[:, q, j, :],
                                                 start=True, stop=True)
                            last.then_inc(s["o_p"], 1)
                schedule(pe, body)

            @block.scalar
            def _(act):
                def body(pair):
                    for g, one, two in steps(pair):
                        if one:
                            q = g.mod(2)
                            w(act, "lwt_p", g)
                            after(act, "o_p", g, -2)
                            act.activation(lw[:, q, :, :], lwt_b[q][:, :, :], ACT.Copy, scale=0.5)\
                                .then_inc(s["lw_ready"], 1)
                        if two:
                            q = g.mod(2, -1)
                            w(act, "o_p", g, -1)
                            after(act, "r3_ready", g, -3)
                            for j in range(G):
                                last = act.activation(act_out[:, q, j, :], o_b[q][:, j, :], ACT.Sigmoid,
                                                      scale=dinv[:, bass.ds(g.at(-1) * G + j, 1)])
                            last.then_inc(s["act_ready"], 1)
                schedule(act, body)

            @block.vector
            def _(dve):
                def body(pair):
                    for g, one, two in steps(pair):
                        if one:
                            after(dve, "lwt_p", g, -2)
                            dve.tensor_copy(h4[:, g.mod(2), :, :],
                                            hs[:, :, bass.ds(g.at() * G, G)].rearrange("p t b -> p b t"))\
                                .then_inc(s["h4_ready"], 1)
                        if two:
                            q = g.mod(2, -1)
                            w(dve, "act_ready", g, -1)
                            after(dve, "y_ready", g, -3)
                            dve.tensor_tensor(r3[:, q, :, :], act_out[:, q, :, :],
                                              xres[:, bass.ds(g.at(-1) * G, G), :], ALU.add)\
                                .then_inc(s["r3_ready"], 1)
                            w(dve, "r3_ready", g, -1)
                            after(dve, "mv_ready", g, -2)
                            for j in range(G):
                                last = dve.bn_stats(stats[:, j, :], r3[:, q, j, :])
                            last.then_inc(s["st_ready"], 1)
                            w(dve, "st_ready", g, -1)
                            after(dve, "rstd_ready", g, -2)
                            after(dve, "y_ready", g, -2)
                            dve.sem_inc(held["DVE"], 1)
                            for j in range(G):
                                last = dve.bn_aggr(mv[:, j, :], stats[:, j, :])
                            last.then_inc(s["mv_ready"], 1)
                            w(dve, "rstd_ready", g, -1)
                            if not (g.static and g.at(-1) < 2):
                                dve.wait_ge(stored[q], g.pair * 16 + 16 * ((g.inner - 1) // 2))
                            for j in range(G):
                                last = dve.tensor_scalar(y[:, q, j, :], r3[:, q, j, :], mv[:, j, 0:1],
                                                         rstd[:, j:j + 1], ALU.subtract, ALU.mult)
                            last.then_inc(s["y_ready"], 1)
                schedule(dve, body)


def lay_out(i):
    c = np.ascontiguousarray
    x, adj = np.asarray(i["x"]), np.asarray(i["adj"])
    offsets, _ = gaussian_constants()
    cols = np.zeros((B, P, ALL_UNITS * R), np.float32)
    cols[:, :, :P] = adj
    L0, L1, L2, L3 = "L0_gnn_", "L1_gnn_", "L2_gnn_", "L3_gnn_"
    g = {n: np.asarray(v) for n, v in i.items()}
    return {
        "x_rows": c(x.transpose(1, 0, 2)),
        "x_cols": c(x.transpose(2, 0, 1)),
        "adj_rows": c(adj.transpose(1, 0, 2)),
        "adj_t": c(adj.transpose(2, 0, 1)),
        "adj_cols": c(cols.reshape(B, P, ALL_UNITS, R).transpose(0, 2, 1, 3)),
        "offsets": c(offsets.reshape(NG, 1)),
        "mask_rows": c(g["nodemask"].T),
        "w1t": c(g[L0 + "W1"].T), "w2t": c(g[L0 + "W2"].T), "wat": c(g[L0 + "Wa"].T),
        "wd1t": c(g[L0 + "Wd1"].T), "wd2t": c(g[L0 + "Wd2"].T),
        "b1c": c(g[L0 + "b1"].reshape(P, 1)), "bd1c": c(g[L0 + "bd1"].reshape(P, 1)),
        "b2row": c(g[L0 + "b2"].reshape(1, P)), "bd2row": c(g[L0 + "bd2"].reshape(1, P)),
        "wq": c(g[L1 + "Wq"]), "wqt": c(g[L1 + "Wq"].T), "wkt": c(g[L1 + "Wk"].T), "wv": c(g[L1 + "Wv"]),
        "gamma_row": c(g[L1 + "gamma"].reshape(1, P)), "beta_row": c(g[L1 + "beta"].reshape(1, P)),
        "w_layer": c(g[L2 + "W_layer"]), "w_layer_t": c(g[L2 + "W_layer"].T),
        "w_self": c(g[L2 + "W_att_self"]), "w_neigh": c(g[L2 + "W_att_neighbor"]),
        "b_layer_row": c(g[L2 + "b_layer"].reshape(1, P)),
        "conv_wt": c(g[L3 + "conv_w"].transpose(1, 2, 0)), "conv_b_row": c(g[L3 + "conv_b"].reshape(1, P)),
        "w_iht": c(g[L3 + "w_ih"].T), "w_hht": c(g[L3 + "w_hh"].T),
        "b_ih_row": c(g[L3 + "b_ih"].reshape(1, 4 * P)), "b_hh_row": c(g[L3 + "b_hh"].reshape(1, 4 * P)),
    }


def kernel(**inputs):
    import concourse.bacc as bacc
    from concourse.bass_utils import run_bass_kernel_spmd

    nc = bacc.Bacc("TRN2", target_bir_lowering=False, num_devices=1)
    arrays = lay_out(inputs)
    aps = {n: nc.dram_tensor(f"in_{n}", v.shape, mybir.dt.from_np(v.dtype), kind="ExternalInput").ap()
           for n, v in arrays.items()}
    out = nc.dram_tensor("out", (B, P, P), F32, kind="ExternalOutput").ap()
    build(nc, aps, out)
    r = run_bass_kernel_spmd(nc, [{f"in_{n}": v for n, v in arrays.items()}], core_ids=[0])
    return r.results[0]["out"]
```
